# Optimizing a Trainium2 kernel written in Bass

```python
import numpy as np
import jax
import jax.numpy as jnp

def _softmax(x, axis=-1):
    return jax.nn.softmax(x, axis=axis)

def _gelu(x):
    return jax.nn.gelu(x, approximate=True)

def _silu(x):
    return jax.nn.silu(x)

def _sigmoid(x):
    return jax.nn.sigmoid(x)

def _layernorm(x, axis=-1, eps=1e-05):
    m = jnp.mean(x, axis=axis, keepdims=True)
    v = jnp.var(x, axis=axis, keepdims=True)
    return (x - m) / jnp.sqrt(v + eps)

def _scatter_add(tgt, idx, src, axis=0):
    return tgt.at[idx].add(src)

def _segment_sum(src, seg, n):
    return jax.ops.segment_sum(src, seg, n)
kernel_name = 'mk_adaln_d1_jaxref_r8_cb75fe'

def setup_inputs(seed: int=0):
    np.random.seed(seed)
    _w = jnp.asarray

    def _L0_attn_setup():
        import jax, jax.numpy as jnp
        import numpy as np
        D_MODEL = 128
        D_INNER = 256
        D_STATE = 16
        DT_RANK = 64
        K_CONV = 4
        D_FF = 512
        EPS = 1e-06

        def _rms(x, w):
            return x * jax.lax.rsqrt(jnp.mean(x * x, axis=-1, keepdims=True) + EPS) * w

        def _reference_tuple_inner(hidden_states, in_proj_w, conv_w, conv_b, x_proj_w, dt_proj_w, dt_proj_b, dt_ln_w, b_ln_w, c_ln_w, A_log, D_skip, out_proj_w, input_ln_w, pre_moe_ln_w, gate_w, up_w, down_w):
            B, S, _ = hidden_states.shape
            residual = hidden_states
            h = _rms(hidden_states, input_ln_w)
            xz = h @ in_proj_w
            x, z = jnp.split(xz, 2, axis=-1)
            xt = jnp.transpose(x, (0, 2, 1))
            conv_state = xt[:, :, -K_CONV:]
            y = jax.lax.conv_general_dilated(xt, conv_w[:, None, :], window_strides=(1,), padding=[(K_CONV - 1, 0)], feature_group_count=D_INNER, dimension_numbers=('NCH', 'OIH', 'NCH'))
            y = y + conv_b[None, :, None]
            x = jax.nn.silu(jnp.transpose(y, (0, 2, 1)))
            proj = x @ x_proj_w
            dt_raw = proj[..., :DT_RANK]
            B_raw = proj[..., DT_RANK:DT_RANK + D_STATE]
            C_raw = proj[..., DT_RANK + D_STATE:]
            dt = jax.nn.softplus(_rms(dt_raw, dt_ln_w) @ dt_proj_w + dt_proj_b)
            Bm = _rms(B_raw, b_ln_w)
            Cm = _rms(C_raw, c_ln_w)
            A = -jnp.exp(A_log)

            def step(hstate, ins):
                x_t, dt_t, B_t, C_t = ins
                dA = jnp.exp(dt_t[..., None] * A)
                hstate = hstate * dA + (dt_t * x_t)[..., None] * B_t[:, None, :]
                y_t = jnp.einsum('bdn,bn->bd', hstate, C_t)
                return (hstate, y_t)
            h0 = jnp.zeros((B, D_INNER, D_STATE), x.dtype)
            xs = (jnp.swapaxes(x, 0, 1), jnp.swapaxes(dt, 0, 1), jnp.swapaxes(Bm, 0, 1), jnp.swapaxes(Cm, 0, 1))
            ssm_state, ys = jax.lax.scan(step, h0, xs)
            y = jnp.swapaxes(ys, 0, 1) + x * D_skip
            y = y * jax.nn.silu(z)
            mamba_out = y @ out_proj_w
            hidden = residual + mamba_out
            residual = hidden
            hn = _rms(hidden, pre_moe_ln_w)
            ff = jax.nn.silu(hn @ gate_w) * (hn @ up_w) @ down_w
            out = residual + ff
            return (out, conv_state, ssm_state)
        key = jax.random.key(seed)
        ks = jax.random.split(key, 20)
        s = lambda i, shape, scale: jax.random.normal(ks[i], shape, dtype=jnp.float32) * scale
        inp = {'hidden_states': s(0, (2, 256, D_MODEL), 1.0), 'in_proj_w': s(1, (D_MODEL, 2 * D_INNER), D_MODEL ** (-0.5)), 'conv_w': s(2, (D_INNER, K_CONV), 0.3), 'conv_b': jnp.zeros((D_INNER,), jnp.float32), 'x_proj_w': s(3, (D_INNER, DT_RANK + 2 * D_STATE), D_INNER ** (-0.5)), 'dt_proj_w': s(4, (DT_RANK, D_INNER), DT_RANK ** (-0.5)), 'dt_proj_b': jnp.full((D_INNER,), -2.0, jnp.float32), 'dt_ln_w': jnp.ones((DT_RANK,), jnp.float32), 'b_ln_w': jnp.ones((D_STATE,), jnp.float32), 'c_ln_w': jnp.ones((D_STATE,), jnp.float32), 'A_log': jnp.log(jnp.broadcast_to(jnp.arange(1, D_STATE + 1, dtype=jnp.float32), (D_INNER, D_STATE))), 'D_skip': jnp.ones((D_INNER,), jnp.float32), 'out_proj_w': s(5, (D_INNER, D_MODEL), D_INNER ** (-0.5)), 'input_ln_w': jnp.ones((D_MODEL,), jnp.float32), 'pre_moe_ln_w': jnp.ones((D_MODEL,), jnp.float32), 'gate_w': s(6, (D_MODEL, D_FF), D_MODEL ** (-0.5)), 'up_w': s(7, (D_MODEL, D_FF), D_MODEL ** (-0.5)), 'down_w': s(8, (D_FF, D_MODEL), D_FF ** (-0.5))}
        return inp
    _L0_attn_in = _L0_attn_setup()

    def _L0_ffn_setup():
        import jax, jax.numpy as jnp
        import numpy as np
        HIDDEN = 128
        INTER = 512
        N_EXPERTS = 8

        def geglu(x, w1, w2, w3):
            return jax.nn.gelu(x @ w1, approximate=False) * (x @ w2) @ w3
        key = jax.random.key(seed)
        ks = jax.random.split(key, 8)
        s = 0.02
        x = jax.random.normal(ks[0], (2, 256, HIDDEN), dtype=jnp.float32)
        w1s = jax.random.normal(ks[1], (HIDDEN, INTER), dtype=jnp.float32) * s
        w2s = jax.random.normal(ks[2], (HIDDEN, INTER), dtype=jnp.float32) * s
        w3s = jax.random.normal(ks[3], (INTER, HIDDEN), dtype=jnp.float32) * s
        W1 = jax.random.normal(ks[4], (N_EXPERTS, HIDDEN, INTER), dtype=jnp.float32) * s
        W2 = jax.random.normal(ks[5], (N_EXPERTS, HIDDEN, INTER), dtype=jnp.float32) * s
        W3 = jax.random.normal(ks[6], (N_EXPERTS, INTER, HIDDEN), dtype=jnp.float32) * s
        Wg = jax.random.normal(ks[7], (HIDDEN, N_EXPERTS), dtype=jnp.float32) * s
        return {'x': x, 'w1s': w1s, 'w2s': w2s, 'w3s': w3s, 'W1': W1, 'W2': W2, 'W3': W3, 'Wg': Wg}
    _L0_ffn_in = _L0_ffn_setup()
    _L0_c = _w((lambda *s: np.random.randn(*s).astype(np.float32) * 0.05)(16, 128))
    _L0_wmod = _w((lambda *s: np.random.randn(*s).astype(np.float32) * 0.05)(128, 6 * 128) * 128 ** (-0.5))
    _d = {'L0_attn_hidden_states': _L0_attn_in['hidden_states'], 'L0_attn_in_proj_w': _L0_attn_in['in_proj_w'], 'L0_attn_conv_w': _L0_attn_in['conv_w'], 'L0_attn_conv_b': _L0_attn_in['conv_b'], 'L0_attn_x_proj_w': _L0_attn_in['x_proj_w'], 'L0_attn_dt_proj_w': _L0_attn_in['dt_proj_w'], 'L0_attn_dt_proj_b': _L0_attn_in['dt_proj_b'], 'L0_attn_dt_ln_w': _L0_attn_in['dt_ln_w'], 'L0_attn_b_ln_w': _L0_attn_in['b_ln_w'], 'L0_attn_c_ln_w': _L0_attn_in['c_ln_w'], 'L0_attn_A_log': _L0_attn_in['A_log'], 'L0_attn_D_skip': _L0_attn_in['D_skip'], 'L0_attn_out_proj_w': _L0_attn_in['out_proj_w'], 'L0_attn_input_ln_w': _L0_attn_in['input_ln_w'], 'L0_attn_pre_moe_ln_w': _L0_attn_in['pre_moe_ln_w'], 'L0_attn_gate_w': _L0_attn_in['gate_w'], 'L0_attn_up_w': _L0_attn_in['up_w'], 'L0_attn_down_w': _L0_attn_in['down_w'], 'L0_ffn_w1s': _L0_ffn_in['w1s'], 'L0_ffn_w2s': _L0_ffn_in['w2s'], 'L0_ffn_w3s': _L0_ffn_in['w3s'], 'L0_ffn_W1': _L0_ffn_in['W1'], 'L0_ffn_W2': _L0_ffn_in['W2'], 'L0_ffn_W3': _L0_ffn_in['W3'], 'L0_ffn_Wg': _L0_ffn_in['Wg'], 'L0_c': _L0_c, 'L0_wmod': _L0_wmod}
    _x0 = _d['L0_attn_hidden_states']
    _d['L0_attn_hidden_states'] = jax.random.normal(jax.random.fold_in(jax.random.key(seed), 1), (16, 256, 128), dtype=_x0.dtype)
    del _x0
    return _d

def reference(L0_attn_hidden_states, L0_attn_in_proj_w, L0_attn_conv_w, L0_attn_conv_b, L0_attn_x_proj_w, L0_attn_dt_proj_w, L0_attn_dt_proj_b, L0_attn_dt_ln_w, L0_attn_b_ln_w, L0_attn_c_ln_w, L0_attn_A_log, L0_attn_D_skip, L0_attn_out_proj_w, L0_attn_input_ln_w, L0_attn_pre_moe_ln_w, L0_attn_gate_w, L0_attn_up_w, L0_attn_down_w, L0_ffn_w1s, L0_ffn_w2s, L0_ffn_w3s, L0_ffn_W1, L0_ffn_W2, L0_ffn_W3, L0_ffn_Wg, L0_c, L0_wmod):

    def _L0_attn_ref(hidden_states, in_proj_w, conv_w, conv_b, x_proj_w, dt_proj_w, dt_proj_b, dt_ln_w, b_ln_w, c_ln_w, A_log, D_skip, out_proj_w, input_ln_w, pre_moe_ln_w, gate_w, up_w, down_w):
        import jax, jax.numpy as jnp
        import numpy as np
        D_MODEL = 128
        D_INNER = 256
        D_STATE = 16
        DT_RANK = 64
        K_CONV = 4
        D_FF = 512
        EPS = 1e-06

        def _rms(x, w):
            return x * jax.lax.rsqrt(jnp.mean(x * x, axis=-1, keepdims=True) + EPS) * w

        def _reference_tuple_inner(hidden_states, in_proj_w, conv_w, conv_b, x_proj_w, dt_proj_w, dt_proj_b, dt_ln_w, b_ln_w, c_ln_w, A_log, D_skip, out_proj_w, input_ln_w, pre_moe_ln_w, gate_w, up_w, down_w):
            B, S, _ = hidden_states.shape
            residual = hidden_states
            h = _rms(hidden_states, input_ln_w)
            xz = h @ in_proj_w
            x, z = jnp.split(xz, 2, axis=-1)
            xt = jnp.transpose(x, (0, 2, 1))
            conv_state = xt[:, :, -K_CONV:]
            y = jax.lax.conv_general_dilated(xt, conv_w[:, None, :], window_strides=(1,), padding=[(K_CONV - 1, 0)], feature_group_count=D_INNER, dimension_numbers=('NCH', 'OIH', 'NCH'))
            y = y + conv_b[None, :, None]
            x = jax.nn.silu(jnp.transpose(y, (0, 2, 1)))
            proj = x @ x_proj_w
            dt_raw = proj[..., :DT_RANK]
            B_raw = proj[..., DT_RANK:DT_RANK + D_STATE]
            C_raw = proj[..., DT_RANK + D_STATE:]
            dt = jax.nn.softplus(_rms(dt_raw, dt_ln_w) @ dt_proj_w + dt_proj_b)
            Bm = _rms(B_raw, b_ln_w)
            Cm = _rms(C_raw, c_ln_w)
            A = -jnp.exp(A_log)

            def step(hstate, ins):
                x_t, dt_t, B_t, C_t = ins
                dA = jnp.exp(dt_t[..., None] * A)
                hstate = hstate * dA + (dt_t * x_t)[..., None] * B_t[:, None, :]
                y_t = jnp.einsum('bdn,bn->bd', hstate, C_t)
                return (hstate, y_t)
            h0 = jnp.zeros((B, D_INNER, D_STATE), x.dtype)
            xs = (jnp.swapaxes(x, 0, 1), jnp.swapaxes(dt, 0, 1), jnp.swapaxes(Bm, 0, 1), jnp.swapaxes(Cm, 0, 1))
            ssm_state, ys = jax.lax.scan(step, h0, xs)
            y = jnp.swapaxes(ys, 0, 1) + x * D_skip
            y = y * jax.nn.silu(z)
            mamba_out = y @ out_proj_w
            hidden = residual + mamba_out
            residual = hidden
            hn = _rms(hidden, pre_moe_ln_w)
            ff = jax.nn.silu(hn @ gate_w) * (hn @ up_w) @ down_w
            out = residual + ff
            return (out, conv_state, ssm_state)
        return _reference_tuple_inner(hidden_states, in_proj_w, conv_w, conv_b, x_proj_w, dt_proj_w, dt_proj_b, dt_ln_w, b_ln_w, c_ln_w, A_log, D_skip, out_proj_w, input_ln_w, pre_moe_ln_w, gate_w, up_w, down_w)[0]

    def _L0_ffn_ref(x, w1s, w2s, w3s, W1, W2, W3, Wg):
        import jax, jax.numpy as jnp
        import numpy as np
        HIDDEN = 128
        INTER = 512
        N_EXPERTS = 8

        def geglu(x, w1, w2, w3):
            return jax.nn.gelu(x @ w1, approximate=False) * (x @ w2) @ w3
        B, T, C = x.shape
        xf = x.reshape(-1, C)
        shared = geglu(xf, w1s, w2s, w3s)
        logits = xf @ Wg
        idx = jnp.argmax(logits, axis=-1)
        final = jnp.zeros_like(xf)
        for e in range(N_EXPERTS):
            y = geglu(xf, W1[e], W2[e], W3[e])
            final = final + jnp.where((idx == e)[:, None], y, 0.0)
        return (shared + final).reshape(B, T, C)
    x = L0_attn_hidden_states
    mod = (_silu(L0_c) @ L0_wmod).reshape(L0_c.shape[0], 6, 1, -1)
    sa, ca, ga, sb, cb, gb = (mod[:, 0], mod[:, 1], mod[:, 2], mod[:, 3], mod[:, 4], mod[:, 5])
    ga = (2 * (ga >= 0) - 1) * jnp.maximum(jnp.abs(ga), 0.25)
    gb = (2 * (gb >= 0) - 1) * jnp.maximum(jnp.abs(gb), 0.25)
    h = _layernorm(x, axis=-1) * (1 + ca) + sa
    x = x + ga * _L0_attn_ref(h, L0_attn_in_proj_w, L0_attn_conv_w, L0_attn_conv_b, L0_attn_x_proj_w, L0_attn_dt_proj_w, L0_attn_dt_proj_b, L0_attn_dt_ln_w, L0_attn_b_ln_w, L0_attn_c_ln_w, L0_attn_A_log, L0_attn_D_skip, L0_attn_out_proj_w, L0_attn_input_ln_w, L0_attn_pre_moe_ln_w, L0_attn_gate_w, L0_attn_up_w, L0_attn_down_w)
    h = _layernorm(x, axis=-1) * (1 + cb) + sb
    x = x + gb * _L0_ffn_ref(h, L0_ffn_w1s, L0_ffn_w2s, L0_ffn_w3s, L0_ffn_W1, L0_ffn_W2, L0_ffn_W3, L0_ffn_Wg)
    return x

_drawn_inputs = setup_inputs


def setup_inputs(seed=0):
    import zlib

    import numpy as np

    out = dict(_drawn_inputs(seed))
    spreads = {'L0_attn_conv_b': (0.0, 0.1),
     'L0_attn_dt_proj_b': (-2.0, 0.6),
     'L0_attn_dt_ln_w': (1.0, 0.6),
     'L0_attn_b_ln_w': (1.0, 0.6),
     'L0_attn_c_ln_w': (1.0, 0.6),
     'L0_attn_D_skip': (1.0, 0.6),
     'L0_attn_input_ln_w': (1.0, 0.2),
     'L0_attn_pre_moe_ln_w': (1.0, 0.2)}
    factors = {'L0_ffn_w1s': 8.0,
     'L0_ffn_w2s': 8.0,
     'L0_ffn_w3s': 8.0,
     'L0_ffn_W1': 8.0,
     'L0_ffn_W2': 8.0,
     'L0_ffn_W3': 8.0,
     'L0_ffn_Wg': 8.0}
    for name, (base, spread) in spreads.items():
        noise = np.random.default_rng([zlib.crc32(name.encode()), seed]).standard_normal(out[name].shape)
        drawn = base * np.exp(spread * noise) if base else spread * noise
        out[name] = jnp.asarray(drawn.astype(out[name].dtype))
    for name, factor in factors.items():
        out[name] = (out[name] * factor).astype(out[name].dtype)
    return out
```

```python
from contextlib import ExitStack

import numpy as np
import concourse.bass as bass
from concourse import mybir

F32 = mybir.dt.float32
BF16 = mybir.dt.bfloat16
U32 = mybir.dt.uint32
I32 = mybir.dt.int32
ALU = mybir.AluOpType
ACT = mybir.ActivationFunctionType
AX = mybir.AxisListType.X

P = 128
B, S, D = 16, 256, 128
DI, NS, R, K = 256, 16, 64, 4
FF = 512
NE = 8
GB = 2
G = B // GB
GT = GB * S
TG = GT // P
NT = B * S // P
H = DI // P
FC = FF // P
XP = R + 2 * NS
BC = 2 * NS
REG = B * S + P
SPARE = NE * REG
TILES = NT + NE
EPS_LN, EPS_RMS = 1e-5, 1e-6

RING_A, RING_X, RING_H, RING_C, RING_P = 4, 2, 2, 2, 2
POOL_N = (0, 2, 4, 6, 8, 10, 12, 14)

WEIGHTS = 16 * 21
POOL_SETUP, DVE_SETUP = 25, 18
GATE_ROWS = 9
A_LINKS, C_LINKS = 12, 16


TABLE_STEPS = (6, 13)
EXP_LN = "natural_log_exp_and_others"


def positive(eng, sem, value):
    if not (isinstance(value, int) and value <= 0):
        eng.wait_ge(sem, value)


def build(nc, io, out):
    ctx = ExitStack()
    with ctx:
        def sb(name, shape, dt=F32):
            return ctx.enter_context(nc.sbuf_tensor(name, shape, dt))

        names = (
            "x_first_in", "x_rest_in", "cond_in", "weights_in", "experts_in", "late_experts_in",
            "pool_setup", "dve_setup", "zeros_out", "silu_c", "silu_ct_ps", "silu_ct", "mod_ps",
            "gate_ps", "gate_read", "exp_a",
            "a0_full", "a1_full", "c0_full", "c1_full",
            "a_dve", "a_act", "a_mv", "a_rstd", "a_xn", "a_h", "a_sq", "a_ln", "a_rms", "a_hn", "a_xpad", "a_conv",
            "a_zs", "a_silu", "a_proj_copy", "a_proj_ms", "a_proj_rs", "a_dtn", "a_parts", "a_dtnt", "bc_parts",
            "a_relu", "a_soft", "dt_ready", "u_ready",
            "b_full", "c_full", "c_copied", "da_ready", "bx_done", "h_done", "hc_dve", "hc_pool", "nsum_done",
            "c_dve", "c_act", "y_read", "yg_ready", "hid_ready", "c_sq", "c_ln", "c_rms", "c_hn", "c_silu", "c_prod",
            "c_sum", "c_scaled", "x2_ready", "c_mv", "c_rstd", "c_n2", "c_h2t", "c_h2tok", "c_eq", "c_onehot",
            "c_counts", "c_slot", "scattered", "c_gelu", "c_sprod", "c_gated", "base_ready",
            "e_dve", "tail_idx", "tails_out", "tables", "xt_in0", "xt_in1", "xt_read", "ext", "up1_ps", "up2_ps",
            "gelu_done", "prod_done", "prodt_ps", "prodt", "down_ps", "yo", "ys_out0", "ys_out1", "gather_idx",
            *(f"gathered{j}" for j in range(G)), "weighted", "final_sum", "out_done",
        )
        s = {n: ctx.enter_context(nc.semaphore(n)) for n in names}

        x_all = sb("x_all", [P, NT, D])
        gate_b = sb("gate_b", [P, B, D])
        w_in = sb("w_in", [P, 2 * DI])
        w_xp = sb("w_xp", [P, H, XP])
        w_dt = sb("w_dt", [R, DI])
        w_out = sb("w_out", [P, H, D])
        w_gate, w_up = sb("w_gate", [P, FF]), sb("w_up", [P, FF])
        w_down = sb("w_down", [P, FC, D])
        w1s, w2s = sb("w1s", [P, FF]), sb("w2s", [P, FF])
        w3s = sb("w3s", [P, FC, D])
        w_route = sb("w_route", [P, NE])
        e_w1 = sb("e_w1", [P, NE, FF])
        sel = sb("sel", [3 * BC, BC], BF16)
        ident, ones = sb("ident", [P, P]), sb("ones", [P, P])
        identb, onesb, tri = sb("identb", [P, P], BF16), sb("onesb", [P, P], BF16), sb("tri", [P, P], BF16)
        mods = sb("mods", [P, 6, B])
        neg_a = sb("neg_a", [P, H, NS])
        conv_w, conv_b = sb("conv_w", [P, H, K]), sb("conv_b", [P, H])
        dt_b, d_skip = sb("dt_b", [P, H]), sb("d_skip", [P, H])
        ln_in, ln_moe, ln_dt = sb("ln_in", [P, 1]), sb("ln_moe", [P, 1]), sb("ln_dt", [R, 1])
        ln_bc = sb("ln_bc", [P, BC])
        eps_ln, eps_rms, one = sb("eps_ln", [P, 1]), sb("eps_rms", [P, 1]), sb("one", [P, 1])
        c_sb, c_silu, c_t = sb("c_sb", [B, D]), sb("c_silu_sb", [B, D]), sb("c_t", [P, B])
        gate16, gate_t1, gate_t2, gate_t3 = (sb(n, [B, D]) for n in ("gate16", "gate_t1", "gate_t2", "gate_t3"))
        mod_t1, mod_t2 = sb("mod_t1", [P, B]), sb("mod_t2", [P, B])

        SHARED = 2 * NE * FF
        shared = sb("a_or_experts", [P, SHARED])
        e_w2 = shared[:, 0:NE * FF].rearrange("p (e f) -> p e f", e=NE)
        e_w3 = shared[:, NE * FF:2 * NE * FF].rearrange("p (e c d) -> p e c d", e=NE, c=FC)
        taken = [0]

        def part(n):
            taken[0] += n
            assert taken[0] <= SHARED
            return shared[:, taken[0] - n:taken[0]]

        xn = part(GT).rearrange("p (t d) -> p t d", t=TG)
        sq_a, rms_a, hn = part(GT), part(GT), part(GT)
        PAD = K - 1 + S
        xpad = part(H * GB * PAD).rearrange("p (h b t) -> p h b t", h=H, b=GB)
        conv = part(H * GT).rearrange("p (h b t) -> p h b t", h=H, b=GB)
        proj_sq = part(TG * XP).rearrange("p (t c) -> p t c", t=TG)
        proj = part(TG * XP).rearrange("p (t c) -> p t c", t=TG)
        dtn = part(TG * R).rearrange("p (t c) -> p t c", t=TG)
        dtn_t = part(GT)
        bcn = part(TG * BC).rearrange("p (t c) -> p t c", t=TG)
        soft = part(H * GT).rearrange("p (h t) -> p h t", h=H)
        relu = part(H * GT).rearrange("p (h t) -> p h t", h=H)

        parts_tok = sb("parts_tok", [P, TG, 3 * BC], BF16)
        a_mod, stats_a, mv_a = sb("a_mod_sb", [P, 2, GB]), sb("stats_a", [P, TG, 6]), sb("mv_a", [P, 3, TG])
        rstd_a, proj_ms, proj_rs = sb("rstd_a", [P, TG]), sb("proj_ms", [P, 3, TG]), sb("proj_rs", [P, 3, TG])
        h_t = sb("h_t", [P, 2, GT])
        parts_t = sb("parts_t", [3 * BC, 2, GT], BF16)
        dt = sb("dt", [P, 2, H, GT])
        NKEEP = 2 * H * GT
        keep = sb("keep", [P, 3 * NKEEP])
        u = keep[:, 0:NKEEP].rearrange("p (q h t) -> p q h t", q=2, h=H)
        xs_ = keep[:, NKEEP:2 * NKEEP].rearrange("p (q h t) -> p q h t", q=2, h=H)
        zs = keep[:, 2 * NKEEP:3 * NKEEP].rearrange("p (q h t) -> p q h t", q=2, h=H)
        y_rows = keep[:, 0:NT * D].rearrange("p (t d) -> p t d", t=NT)

        da = sb("da", [P, RING_A, H, GB, S])
        bx = sb("bx", [P, RING_X, H, GT])
        hs = sb("hs", [P, RING_H, H, GT])
        cs = sb("cs", [P, RING_C, GT])
        hc = sb("hc", [P, RING_P, H, GT])

        c_mod = sb("c_mod_sb", [P, 6, GB])
        hid, tmp_c, rms_c = sb("hid", [P, GT]), sb("tmp_c", [P, GT]), sb("rms_c", [P, GT])
        act_c = sb("act_c", [P, 2, GT])
        prod_c = sb("prod_c", [P, FC, GT])
        yt = prod_c[:, 0:H, :]
        wmod = prod_c[:, :, :].rearrange("p c t -> p (c t)")[:, 0:6 * D]
        n2 = tmp_c[:, :].rearrange("p (t d) -> p t d", t=TG)
        h2_t, h2_tok = sb("h2_t", [P, GT]), sb("h2_tok", [P, TG, D])
        stats_c, mv_c, rstd_c = sb("stats_c", [P, TG, 6]), sb("mv_c", [P, 3, TG]), sb("rstd_c", [P, TG])
        lmax, eq, rev = sb("lmax", [P, TG]), sb("eq", [P, TG, NE]), sb("rev", [P, NE])
        emax, onehot = sb("emax", [P, TG]), sb("onehot", [P, TG, NE], BF16)
        base5, rk, rank = sb("base5", [P, TG + 1, NE]), sb("rk", [P, TG, NE]), sb("rank", [P, TG])
        slot_f, slot = sb("slot_f", [P, TG]), sb("slot", [P, TG], U32)
        onehot_all, rank_all = sb("onehot_all", [P, NT, NE], BF16), sb("rank_all", [P, NT])

        iota_k, iota_j = sb("iota_k", [P, NT]), sb("iota_j", [P, TILES])
        iota_i = sb("iota_i", [P, TILES], I32)
        region, pid = sb("region", [P, NE]), sb("pid", [P, 1])
        zeros = sb("zeros", [P, D])
        big = sb("big", [P, TILES, NE])
        n_tiles, last_tile, first_tile = sb("n_tiles", [P, NE]), sb("last_tile", [P, NE]), sb("first_tile", [P, NE])
        ones8 = sb("ones8", [P, NE])
        ej, kj, vj, rowf = sb("ej", [P, TILES]), sb("kj", [P, TILES]), sb("vj", [P, TILES]), sb("rowf", [P, TILES])
        row_tab, exp_tab = sb("row_tab", [P, TILES], I32), sb("exp_tab", [P, TILES], I32)
        tail_f, tail = sb("tail_f", [P, NE]), sb("tail", [P, NE], U32)
        gidx_f, gidx = sb("gidx_f", [P, NT]), sb("gidx", [P, NT], U32)

        ring = hs[:, :, :, :].rearrange("p r h t -> p (r h t)")
        xt = ring[:, 0:2 * P].rearrange("p (r d) -> p r d", r=2)
        ext = ring[:, 2 * P:4 * P].rearrange("p (r d) -> p r d", r=2)
        yo = ring[:, 4 * P:6 * P].rearrange("p (r d) -> p r d", r=2)
        ring2 = da[:, :, :, :, :].rearrange("p r h b t -> p (r h b t)")
        gel = ring2[:, 0:2 * FF].rearrange("p (r f) -> p r f", r=2)
        pe_ = ring2[:, 2 * FF:4 * FF].rearrange("p (r f) -> p r f", r=2)
        pet = ring2[:, 4 * FF:6 * FF].rearrange("p (r f) -> p r f", r=2)

        bank = [ctx.enter_context(nc.psum_tensor(f"bank{i}", [P, 512], F32)) for i in range(8)]
        BB, BCC, Y, AW, CW = bank[0], bank[1], bank[2:4], bank[4:6], bank[6:8]

        xs_rows = nc.dram_tensor("xs_rows", (SPARE + P, D), F32, kind="Internal").ap()
        ys_rows = nc.dram_tensor("ys_rows", (TILES * P, D), F32, kind="Internal").ap()

        A_FREED = [("a_h", 1, 1), ("a_ln", 1, 1), ("a_xpad", 2, 1), ("a_xpad", 2, 2), ("a_zs", 2, 1), ("a_zs", 2, 2),
                   ("a_proj_copy", 1, 1), ("a_dtnt", 1, 1), ("bc_parts", 1, 1), ("a_relu", 2, 1), ("a_relu", 2, 2)]
        C_FREED = [("hid_ready", 1, 1), ("c_ln", 1, 1), ("c_silu", 4, 1), ("c_silu", 4, 2), ("c_prod", 4, 1),
                   ("c_prod", 4, 2), ("c_silu", 4, 3), ("c_silu", 4, 4), ("c_prod", 4, 3), ("c_prod", 4, 4),
                   ("c_sum", 1, 1), ("x2_ready", 1, 1), ("c_h2t", 1, 1), ("c_h2tok", 1, 1), ("c_eq", 1, 1),
                   ("c_gelu", 4, 1), ("c_gelu", 4, 2), ("c_sprod", 4, 1), ("c_sprod", 4, 2), ("c_gelu", 4, 3),
                   ("c_gelu", 4, 4), ("c_sprod", 4, 3), ("c_sprod", 4, 4), ("c_counts", 1, 1), ("c_gated", 1, 1)]

        def take(pe, uses, i, j):
            if i < 2:
                i, j = max(k for k in range(len(uses)) if k % 2 == i % 2) , j - 1
            else:
                i -= 2
            name, per, count = uses[i]
            positive(pe, s[name], j * per + count)

        def filled(eng, chain, uses, i, j):
            in_group = (len(uses) + 1 - i % 2) // 2
            eng.wait_ge(s[f"{chain}{i % 2}_full"], j * in_group + i // 2 + 1)

        A_XNT, A_SSQ, A_X, A_Z, A_PROJ, A_DTT, A_BCT, A_DT = 0, 1, 2, 4, 6, 7, 8, 9
        (C_OUT, C_SSQ, C_G01, C_U01, C_G23, C_U23, C_DOWN, C_OGT, C_N2T, C_BACK, C_LOGIT,
         C_V01, C_W01, C_V23, C_W23, C_RANK, C_SHARED) = 0, 1, 2, 4, 6, 8, 10, 11, 12, 13, 14, 15, 17, 19, 21, 23, 24

        def chained(eng, name, per_group):
            done = [0]

            def link(j, ins):
                i = done[0] % per_group
                done[0] += 1
                ins.then_inc(s[name], 1)
                eng.wait_ge(s[name], j * per_group + i + 1)
            return link

        def apart(eng):
            eng.wait_ge(s["pool_setup"], POOL_SETUP)

        def hc_of(g, n):
            dve_n = [m for m in range(NS) if m not in POOL_N]
            if n in POOL_N:
                return s["hc_pool"], g * len(POOL_N) + POOL_N.index(n) + 1
            return s["hc_dve"], g * len(dve_n) + dve_n.index(n) + 1

        def back(g, n, k):
            g, n = (g, n - k) if n >= k else (g - 1, n - k + NS)
            return None if isinstance(g, int) and g < 0 else (g, n)

        def wait_hc(eng, step):
            if step is not None:
                eng.wait_ge(*hc_of(*step))

        def groups(eng, body):
            body(0, 0, True, False)
            with eng.Fori(0, (G - 2) // 2) as i:
                body(2 * i + 1, 1, True, True)
                body(2 * i + 2, 0, True, True)
            body(G - 1, (G - 1) % 2, False, True)

        block = ctx.enter_context(nc.Block())

        @block.sync
        def _(sp):
            def load(dst, src, sem):
                sp.dma_start(dst, src).then_inc(s[sem], 16)

            x_v = io["L0_attn_hidden_states"].rearrange("b (t p) d -> p (b t) d", p=P)
            load(x_all[:, 0:TG, :], x_v[:, 0:TG, :], "x_first_in")
            load(c_sb[:, :], io["L0_c"], "cond_in")
            load(wmod, io["L0_wmod"], "cond_in")
            small = [
                (w_in[:, :], io["L0_attn_in_proj_w"]),
                (ln_in[:, :], io["L0_attn_input_ln_w"].rearrange("(p o) -> p o", o=1)),
                (conv_w[:, :, :], io["L0_attn_conv_w"].rearrange("(h p) k -> p h k", p=P)),
                (conv_b[:, :], io["L0_attn_conv_b"]),
                (w_xp[:, :, :], io["L0_attn_x_proj_w"].rearrange("(h p) c -> p h c", p=P)),
                (ln_dt[:, :], io["L0_attn_dt_ln_w"].rearrange("(p o) -> p o", o=1)),
                (ln_bc[:, 0:NS], io["L0_attn_b_ln_w"].partition_broadcast(P)),
                (ln_bc[:, NS:BC], io["L0_attn_c_ln_w"].partition_broadcast(P)),
                (w_dt[:, :], io["L0_attn_dt_proj_w"]),
                (dt_b[:, :], io["L0_attn_dt_proj_b"]),
                (neg_a[:, :, :], io["L0_attn_A_log"].rearrange("(h p) n -> p h n", p=P)),
                (d_skip[:, :], io["L0_attn_D_skip"]),
                (w_out[:, :, :], io["L0_attn_out_proj_w"].rearrange("(h p) d -> p h d", p=P)),
                (ln_moe[:, :], io["L0_attn_pre_moe_ln_w"].rearrange("(p o) -> p o", o=1)),
                (w_gate[:, :], io["L0_attn_gate_w"]),
                (w_up[:, :], io["L0_attn_up_w"]),
                (w_down[:, :, :], io["L0_attn_down_w"].rearrange("(c p) d -> p c d", p=P)),
                (w1s[:, :], io["L0_ffn_w1s"]),
                (w2s[:, :], io["L0_ffn_w2s"]),
                (w3s[:, :, :], io["L0_ffn_w3s"].rearrange("(c p) d -> p c d", p=P)),
                (w_route[:, :], io["L0_ffn_Wg"]),
            ]
            assert 16 * len(small) == WEIGHTS
            for dst, src in small:
                load(dst, src, "weights_in")
            for j in range(1, G):
                load(x_all[:, j * TG:(j + 1) * TG, :], x_v[:, j * TG:(j + 1) * TG, :], "x_rest_in")
            for e in range(NE):
                load(e_w1[:, e, :], io["L0_ffn_W1"][e, :, :], "experts_in")
            sp.wait_ge(s["pool_setup"], POOL_SETUP)
            load(xs_rows[SPARE:SPARE + P, :], zeros[:, :], "zeros_out")

            sp.wait_ge(s["u_ready"], G)
            sp.wait_ge(s["bc_parts"], G)
            for e in range(NE):
                load(e_w2[:, e, :], io["L0_ffn_W2"][e, :, :], "late_experts_in")
                load(e_w3[:, e, :, :], io["L0_ffn_W3"][e, :, :].rearrange("(c p) d -> p c d", p=P), "late_experts_in")

            sp.wait_ge(s["tables"], 1)
            sp.wait_ge(s["scattered"], 16 * NT)
            sp.wait_ge(s["tails_out"], 16 * NE)
            sp.wait_ge(s["zeros_out"], 16)

            def load_tile(i, r):
                row = sp.value_load(row_tab[0:1, bass.ds(2 * i + r, 1)], min_val=0, max_val=SPARE)
                positive(sp, s["xt_read"], 2 * i + r - 1)
                sp.dma_start(xt[:, r, :], xs_rows[bass.ds(row, P), :]).then_inc(s[f"xt_in{r}"], 16)

            for r in range(2):
                load_tile(0, r)
            with sp.Fori(1, TILES // 2) as i:
                for r in range(2):
                    load_tile(i, r)

            out_v = out.rearrange("b (t p) d -> p (b t) d", p=P)
            for j in range(G):
                sp.wait_ge(s["final_sum"], j + 1)
                sp.dma_start(out_v[:, j * TG:(j + 1) * TG, :], x_all[:, j * TG:(j + 1) * TG, :]).then_inc(s["out_done"], 16)
            sp.wait_ge(s["out_done"], 16 * G)


        @block.gpsimd
        def _(pool):
            count = [0]

            def setup(ins):
                count[0] += 1
                ins.then_inc(s["pool_setup"], 1)
                pool.wait_ge(s["pool_setup"], count[0])

            def diagonal(t, base, cols):
                setup(pool.affine_select(out=t, in_=t, compare_op=ALU.not_equal, fill=1.0, base=-base,
                                         pattern=[[-1, cols]], channel_multiplier=1))

            setup(pool.memset(ident[:, :], 0.0))
            diagonal(ident[:, :], 0, P)
            setup(pool.memset(eps_ln[:, :], EPS_LN))
            setup(pool.memset(eps_rms[:, :], EPS_RMS))
            setup(pool.memset(one[:, :], 1.0))
            setup(pool.memset(ones[:, :], 1.0))
            setup(pool.memset(identb[:, :], 0.0))
            diagonal(identb[:, :], 0, P)
            setup(pool.memset(sel[:, :], 0.0))
            for k in range(3):
                diagonal(sel[:, :], BC * k, BC)
            setup(pool.memset(onesb[:, :], 1.0))
            setup(pool.memset(tri[:, :], 1.0))
            setup(pool.affine_select(out=tri[:, :], in_=tri[:, :], compare_op=ALU.is_gt, fill=0.0, base=0,
                                     pattern=[[1, P]], channel_multiplier=-1))
            setup(pool.memset(zeros[:, :], 0.0))
            setup(pool.memset(ones8[:, :], 1.0))
            setup(pool.memset(base5[:, :, :], 0.0))
            setup(pool.iota(iota_i[:, :], [[1, TILES]], base=0, channel_multiplier=0))
            setup(pool.tensor_copy(iota_j[:, :], iota_i[:, :]))
            setup(pool.iota(iota_i[:, 0:1], [[1, 1]], base=0, channel_multiplier=1))
            setup(pool.tensor_copy(pid[:, :], iota_i[:, 0:1]))
            setup(pool.tensor_scalar(iota_k[:, :], iota_j[:, 0:NT], float(P), None, ALU.mult))
            setup(pool.tensor_scalar(region[:, :], iota_j[:, 0:NE], float(REG), None, ALU.mult))
            setup(pool.tensor_scalar(rev[:, :], iota_j[:, 0:NE], -1.0, float(NE), ALU.mult, ALU.add))
            assert count[0] == POOL_SETUP

            def scan(g, q, n):
                if n not in POOL_N:
                    return
                pool.wait_ge(s["c_copied"], g * NS + n + 1)
                pool.wait_ge(s["h_done"], g * NS + n + 1)
                positive(pool, s["nsum_done"], g * NS + n - RING_P + 1)
                pool.tensor_tensor(hc[:, n % RING_P], hs[:, n % RING_H],
                                   cs[:, n % RING_C].unsqueeze(1).broadcast_to([P, H, GT]), ALU.mult)\
                    .then_inc(s["hc_pool"], 1)

            def c_scatter(j):
                apart(pool)
                pool.wait_ge(s["c_slot"], j + 1)
                pool.wait_ge(s["c_h2tok"], j + 1)
                for t in range(TG):
                    pool.indirect_dma_start(out=xs_rows, out_offset=bass.IndirectOffsetOnAxis(ap=slot[:, t:t + 1], axis=0),
                                            in_=h2_tok[:, t, :], in_offset=None).then_inc(s["scattered"], 16)

            def body(g, q, has_a, has_c):
                for n in range(NS):
                    scan(g, q, n)
                    if has_c and n == 15:
                        c_scatter(g - 1)

            groups(pool, body)
            c_scatter(G - 1)

            pool.wait_ge(s["tail_idx"], 1)
            for e in range(NE):
                pool.indirect_dma_start(out=xs_rows, out_offset=bass.IndirectOffsetOnAxis(ap=tail[:, e:e + 1], axis=0),
                                        in_=zeros[:, :], in_offset=None).then_inc(s["tails_out"], 16)

            def store(i, r):
                pool.wait_ge(s["yo"], 2 * i + r + 1)
                pool.dma_start(ys_rows[bass.ds((2 * i + r) * P, P), :], yo[:, r, :]).then_inc(s[f"ys_out{r}"], 16)

            with pool.Fori(0, TILES // 2) as i:
                for r in range(2):
                    store(i, r)
            for r in range(2):
                pool.wait_ge(s[f"ys_out{r}"], 16 * (TILES // 2))
            pool.wait_ge(s["gather_idx"], 1)
            pool.wait_ge(s["nsum_done"], G * NS)
            for t in range(NT):
                pool.indirect_dma_start(out=y_rows[:, t, :], out_offset=None, in_=ys_rows,
                                        in_offset=bass.IndirectOffsetOnAxis(ap=gidx[:, t:t + 1], axis=0))\
                    .then_inc(s[f"gathered{t // TG}"], 16)

        @block.tensor
        def _(pe):
            mm = pe.matmul

            pe.wait_ge(s["pool_setup"], POOL_SETUP)
            pe.wait_ge(s["silu_c"], 1)
            pe.transpose(Y[0][:, 0:B], c_silu[:, :], ident[0:B, 0:B]).then_inc(s["silu_ct_ps"], 1)
            pe.wait_ge(s["silu_ct"], 1)
            pe.wait_ge(s["cond_in"], 32)
            for m in range(6):
                mm(Y[0][:, m * B:(m + 1) * B], wmod[:, m * D:(m + 1) * D], c_t[:, :], start=True, stop=True)
            mm(Y[0][0:B, P:P + D], c_t[:, :], wmod[:, 5 * D:6 * D], start=True, stop=True).then_inc(s["mod_ps"], 1)
            pe.wait_ge(s["dve_setup"], GATE_ROWS)
            for r in range(B // 4):
                positive(pe, s["gate_read"], r - 1)
                for b in range(4):
                    last = mm(Y[(r + 1) % 2][:, b * D:(b + 1) * D], ident[0:B, 4 * r + b:4 * r + b + 1].broadcast_to([B, P]),
                              gate16[:, :], start=True, stop=True)
                last.then_inc(s["gate_ps"], 1)
            pe.wait_ge(s["weights_in"], WEIGHTS)
            pe.wait_ge(s["dve_setup"], DVE_SETUP)
            pe.wait_ge(s["gate_read"], B // 4)

            def a_take(i, j):
                take(pe, A_FREED, i, j)
                return AW[i % 2]

            def c_take(i, j):
                take(pe, C_FREED, i, j)
                return CW[i % 2]

            def a_xnt(j):
                pe.wait_ge(s["a_xn"], j + 1)
                w = a_take(A_XNT, j)
                for t in range(TG):
                    last = pe.transpose(w[:, t * P:(t + 1) * P], xn[:, t, :], ident[:, :])
                last.then_inc(s["a0_full"], 1)

            def a_ssq(j):
                pe.wait_ge(s["a_sq"], j + 1)
                mm(a_take(A_SSQ, j)[:, :], ones[:, :], sq_a, start=True, stop=True).then_inc(s["a1_full"], 1)

            def a_in(j, first):
                pe.wait_ge(s["a_hn"], j + 1)
                for h in range(2):
                    c = h if first == A_X else 2 + h
                    mm(a_take(first + h, j)[:, :], w_in[:, c * P:(c + 1) * P], hn, start=True, stop=True)\
                        .then_inc(s[f"a{h}_full"], 1)

            def a_proj(j, q):
                pe.wait_ge(s["a_silu"], j + 1)
                w = a_take(A_PROJ, j)
                for t in range(TG):
                    for h in range(H):
                        last = mm(w[:, t * XP:(t + 1) * XP], xs_[:, q, h, t * P:(t + 1) * P], w_xp[:, h, :],
                                  start=(h == 0), stop=(h == H - 1))
                last.then_inc(s["a0_full"], 1)

            def a_dtbc_t(j):
                apart(pe)
                pe.wait_ge(s["a_dtn"], j + 1)
                w = a_take(A_DTT, j)
                for t in range(TG):
                    last = pe.transpose(w[0:R, t * P:(t + 1) * P], dtn[:, t, :], ident[:, :])
                last.then_inc(s["a1_full"], 1)
                pe.wait_ge(s["a_parts"], j + 1)
                wb = a_take(A_BCT, j)[:, :].bitcast(BF16)
                for t in range(TG):
                    last = pe.transpose(wb[0:3 * BC, t * P:(t + 1) * P], parts_tok[:, t, :], identb[:, :])
                last.then_inc(s["a0_full"], 1)

            def a_dt(j):
                pe.wait_ge(s["a_dtnt"], j + 1)
                for h in range(H):
                    mm(a_take(A_DT + h, j)[:, :], w_dt[:, h * P:(h + 1) * P], dtn_t[0:R, :], start=True, stop=True)\
                        .then_inc(s[f"a{(A_DT + h) % 2}_full"], 1)

            def run_a(n, j, q):
                if n == 2:
                    a_xnt(j)
                if n == 3:
                    a_ssq(j)
                if n == 5:
                    a_in(j, A_X)
                    a_in(j, A_Z)
                if n == 8:
                    a_proj(j, q)
                if n == 10:
                    a_dtbc_t(j)
                if n == 11:
                    a_dt(j)

            def c_out(j):
                pe.wait_ge(s["yg_ready"], j + 1)
                w = c_take(C_OUT, j)
                for h in range(H):
                    last = mm(w[:, :], w_out[:, h, :], yt[:, h, :], start=(h == 0), stop=(h == H - 1))
                last.then_inc(s["c0_full"], 1)

            def c_ssq(j):
                pe.wait_ge(s["c_sq"], j + 1)
                mm(c_take(C_SSQ, j)[:, :], ones[:, :], tmp_c[:, :], start=True, stop=True).then_inc(s["c1_full"], 1)

            def c_pair(j, use, w, f, rhs):
                for k in range(2):
                    mm(c_take(use + k, j)[:, :], w[:, (f + k) * P:(f + k + 1) * P], rhs, start=True, stop=True)\
                        .then_inc(s[f"c{(use + k) % 2}_full"], 1)

            def c_down(j):
                pe.wait_ge(s["c_prod"], j * FC + FC)
                w = c_take(C_DOWN, j)
                for f in range(FC):
                    last = mm(w[:, :], w_down[:, f, :], prod_c[:, f, :], start=(f == 0), stop=(f == FC - 1))
                last.then_inc(s["c0_full"], 1)

            def c_ogt(j):
                pe.wait_ge(s["c_scaled"], j + 1)
                w = c_take(C_OGT, j)
                for t in range(TG):
                    last = pe.transpose(w[:, t * P:(t + 1) * P], act_c[:, 0, t * P:(t + 1) * P], ident[:, :])
                last.then_inc(s["c1_full"], 1)

            def c_n2t(j):
                pe.wait_ge(s["c_n2"], j + 1)
                w = c_take(C_N2T, j)
                for t in range(TG):
                    last = pe.transpose(w[:, t * P:(t + 1) * P], n2[:, t, :], ident[:, :])
                last.then_inc(s["c0_full"], 1)

            def c_back_logit(j):
                pe.wait_ge(s["c_h2t"], j + 1)
                w = c_take(C_BACK, j)
                for t in range(TG):
                    last = pe.transpose(w[:, t * P:(t + 1) * P], h2_t[:, t * P:(t + 1) * P], ident[:, :])
                last.then_inc(s["c1_full"], 1)
                w = c_take(C_LOGIT, j)
                for t in range(TG):
                    last = mm(w[:, t * NE:(t + 1) * NE], h2_t[:, t * P:(t + 1) * P], w_route[:, :], start=True, stop=True)
                last.then_inc(s["c0_full"], 1)

            def c_rank(j):
                pe.wait_ge(s["c_onehot"], j + 1)
                w = c_take(C_RANK, j)
                oh = onehot[:, :, :].rearrange("p t e -> p (t e)")
                mm(w[:, 0:TG * NE], tri[:, :], oh, start=True, stop=True)
                mm(w[:, TG * NE:2 * TG * NE], onesb[:, :], oh, start=True, stop=True).then_inc(s["c1_full"], 1)

            def c_shared(j):
                pe.wait_ge(s["c_sprod"], j * FC + FC)
                w = c_take(C_SHARED, j)
                for t in range(TG):
                    for f in range(FC):
                        last = mm(w[:, t * D:(t + 1) * D], prod_c[:, f, t * P:(t + 1) * P], w3s[:, f, :],
                                  start=(f == 0), stop=(f == FC - 1))
                last.then_inc(s["c0_full"], 1)

            def run_c(n, j):
                if n == 2:
                    c_out(j)
                if n == 3:
                    c_ssq(j)
                if n == 5:
                    pe.wait_ge(s["c_hn"], j + 1)
                    c_pair(j, C_G01, w_gate, 0, tmp_c[:, :])
                if n == 6:
                    c_pair(j, C_U01, w_up, 0, tmp_c[:, :])
                if n == 7:
                    c_pair(j, C_G23, w_gate, 2, tmp_c[:, :])
                    c_pair(j, C_U23, w_up, 2, tmp_c[:, :])
                if n == 9:
                    c_down(j)
                if n == 10:
                    c_ogt(j)
                if n == 12:
                    c_n2t(j)
                    c_back_logit(j)
                if n == 13:
                    c_pair(j, C_V01, w1s, 0, h2_t[:, :])
                    c_pair(j, C_W01, w2s, 0, h2_t[:, :])
                if n == 14:
                    c_pair(j, C_V23, w1s, 2, h2_t[:, :])
                    c_pair(j, C_W23, w2s, 2, h2_t[:, :])
                if n == 15:
                    c_rank(j)
                    c_shared(j)

            def sum_state(g, n):
                wait_hc(pe, (g, n))
                if n == 0:
                    positive(pe, s["y_read"], g)
                for h in range(H):
                    last = mm(Y[h][:, :], ident[:, :], hc[:, n % RING_P, h, :], start=(n == 0), stop=(n == NS - 1))
                last.then_inc(s["nsum_done"], 1)

            def b_row(g, q, n):
                if n == 0:
                    pe.wait_ge(s["bc_parts"], g + 1)
                positive(pe, s["bx_done"], g * NS + n)
                mm(BB[:, :], sel[:, n:n + 1].broadcast_to([3 * BC, P]), parts_t[:, q, :], start=True, stop=True)\
                    .then_inc(s["b_full"], 1)

            def c_row(g, q, n):
                positive(pe, s["c_copied"], g * NS + n)
                mm(BCC[:, :], sel[:, NS + n:NS + n + 1].broadcast_to([3 * BC, P]), parts_t[:, q, :],
                   start=True, stop=True).then_inc(s["c_full"], 1)

            def body(g, q, has_a, has_c):
                for n in range(NS):
                    if n + 1 < NS:
                        b_row(g, q, n + 1)
                    elif has_a:
                        b_row(g + 1, 1 - q, 0)
                    for k in {0: (2, 1), 1: ()}.get(n, (2,)):
                        step = back(g, n, k)
                        if step is not None:
                            sum_state(*step)
                    if n + 1 < NS:
                        c_row(g, q, n + 1)
                    elif has_a:
                        c_row(g + 1, 1 - q, 0)
                    if has_c:
                        run_c(n, g - 1)
                    if has_a:
                        run_a(n, g + 1, 1 - q)

            for n in range(NS):
                run_a(n, 0, 0)
            b_row(0, 0, 0)
            c_row(0, 0, 0)
            groups(pe, body)
            sum_state(G - 1, NS - 2)
            sum_state(G - 1, NS - 1)
            for n in range(NS):
                run_c(n, G - 1)

            XT_B, PT_B, DOWN_B = bank[0], bank[1], bank[2]
            UP1, UP2 = bank[3:5], bank[5:7]

            def e_transpose(i, r):
                pe.wait_ge(s[f"xt_in{r}"], 16 * i + 16)
                positive(pe, s["ext"], 2 * i + r)
                pe.transpose(XT_B[:, 0:P], xt[:, r, :], ident[:, :]).then_inc(s["xt_read"], 1)

            def e_up(i, r, w, banks, done, freed, e):
                positive(pe, s[freed], 2 * i + r - 1)
                mm(banks[r][:, :], ext[:, r, :], w[:, bass.ds(e, 1), :].rearrange("p o f -> p (o f)"),
                   start=True, stop=True).then_inc(s[done], 1)

            def e_prod_t(i, r):
                pe.wait_ge(s["prod_done"], 2 * i + r + 1)
                positive(pe, s["prodt"], 2 * i + r)
                for f in range(FC):
                    last = pe.transpose(PT_B[:, f * P:(f + 1) * P], pe_[:, r, f * P:(f + 1) * P], ident[:, :])
                last.then_inc(s["prodt_ps"], 1)

            def e_down(i, r, e):
                pe.wait_ge(s["prodt"], 2 * i + r + 1)
                positive(pe, s["yo"], 2 * i + r)
                for f in range(FC):
                    last = mm(DOWN_B[:, 0:D], pet[:, r, f * P:(f + 1) * P],
                              e_w3[:, bass.ds(e, 1), f, :].rearrange("p o d -> p (o d)"), start=(f == 0), stop=(f == FC - 1))
                last.then_inc(s["down_ps"], 1)

            def expert_of(i, r):
                return pe.value_load(exp_tab[0:1, bass.ds(2 * i + r, 1)], min_val=0, max_val=NE - 1)

            def e_step(i, r, following, before):
                if following is not None:
                    e_transpose(*following)
                e = expert_of(i, r)
                pe.wait_ge(s["ext"], 2 * i + r + 1)
                e_up(i, r, e_w1, UP1, "up1_ps", "gelu_done", e)
                if before is not None:
                    e_prod_t(*before)
                e_up(i, r, e_w2, UP2, "up2_ps", "prod_done", e)
                if before is not None:
                    e_down(*before, expert_of(*before))

            pe.wait_ge(s["tables"], 1)
            pe.wait_ge(s["experts_in"], 16 * NE)
            pe.wait_ge(s["late_experts_in"], 32 * NE)
            pe.wait_ge(s["base_ready"], G)
            e_transpose(0, 0)
            e_step(0, 0, (0, 1), None)
            with pe.Fori(0, TILES // 2 - 1) as i:
                e_step(i, 1, (i + 1, 0), (i, 0))
                e_step(i + 1, 0, (i + 1, 1), (i, 1))
            L = TILES // 2 - 1
            e_step(L, 1, None, (L, 0))
            e_prod_t(L, 1)
            e_down(L, 1, expert_of(L, 1))

        @block.scalar
        def _(act):
            f = act.activation

            act.wait_ge(s["cond_in"], 32)
            f(c_silu[:, :], c_sb[:, :], ACT.Silu).then_inc(s["silu_c"], 1)
            act.wait_ge(s["silu_ct_ps"], 1)
            f(c_t[:, :], Y[0][:, 0:B], ACT.Copy).then_inc(s["silu_ct"], 1)
            act.wait_ge(s["weights_in"], WEIGHTS)
            act.preload_act_table_set(EXP_LN)
            f(neg_a[:, :, :], neg_a[:, :, :], ACT.Exp).then_inc(s["exp_a"], 1)
            act.wait_ge(s["pool_setup"], POOL_SETUP)
            act.wait_ge(s["dve_setup"], DVE_SETUP)

            link_a = chained(act, "a_act", 3)
            link_c = chained(act, "c_act", 1)

            def a_rstd(j):
                act.wait_ge(s["a_mv"], j + 1)
                link_a(j, f(rstd_a[:, :], mv_a[:, 1, :], ACT.Ln, scale=1.0 / D, bias=eps_ln[:, :]))
                f(rstd_a[:, :], rstd_a[:, :], ACT.Exp, scale=-0.5).then_inc(s["a_rstd"], 1)

            def a_h(j, q):
                filled(act, "a", A_FREED, A_XNT, j)
                positive(act, s["hid_ready"], j - 1)
                for b in range(GB):
                    last = f(h_t[:, q, b * S:(b + 1) * S], AW[0][:, b * S:(b + 1) * S], ACT.Identity,
                             scale=a_mod[:, 1, b:b + 1], bias=a_mod[:, 0, b:b + 1])
                last.then_inc(s["a_h"], 1)
                act.wait_ge(s["a_h"], j + 1)
                f(sq_a, h_t[:, q, :], ACT.Square).then_inc(s["a_sq"], 1)

            def a_rms(j):
                filled(act, "a", A_FREED, A_SSQ, j)
                positive(act, s["a_hn"], j)
                f(rms_a, AW[1][:, :], ACT.Ln, scale=1.0 / D, bias=eps_rms[:, :]).then_inc(s["a_ln"], 1)
                act.wait_ge(s["a_ln"], j + 1)
                f(rms_a, rms_a, ACT.Exp, scale=-0.5).then_inc(s["a_rms"], 1)

            def a_xcopy(j):
                positive(act, s["a_conv"], j)
                for h in range(H):
                    filled(act, "a", A_FREED, A_X + h, j)
                    f(xpad[:, h, :, K - 1:PAD], AW[h][:, :].rearrange("p (b t) -> p b t", b=GB), ACT.Copy)\
                        .then_inc(s["a_xpad"], 1)

            def a_silu_z(j, q):
                positive(act, s["yg_ready"], j - 1)
                for h in range(H):
                    filled(act, "a", A_FREED, A_Z + h, j)
                    f(zs[:, q, h, :], AW[h][:, :], ACT.Silu).then_inc(s["a_zs"], 1)

            def a_silu_x(j, q):
                act.wait_ge(s["a_conv"], j + 1)
                f(xs_[:, q, :, :].rearrange("p h t -> p (h t)"), conv.rearrange("p h b t -> p (h b t)"), ACT.Silu)\
                    .then_inc(s["a_silu"], 1)

            def a_proj_copy(j):
                filled(act, "a", A_FREED, A_PROJ, j)
                w = AW[0][:, 0:TG * XP].rearrange("p (t c) -> p t c", t=TG)
                f(proj_sq, w, ACT.Square)
                f(proj, w, ACT.Copy).then_inc(s["a_proj_copy"], 1)

            def a_proj_rs(j):
                act.wait_ge(s["a_proj_ms"], j + 1)
                f(proj_rs[:, 0, :], proj_ms[:, 0, :], ACT.Ln, scale=1.0 / R, bias=eps_rms[:, :])
                link_a(j, f(proj_rs[:, 1:3, :], proj_ms[:, 1:3, :], ACT.Ln, scale=1.0 / NS, bias=eps_rms[:, :]))
                f(proj_rs[:, :, :], proj_rs[:, :, :], ACT.Exp, scale=-0.5).then_inc(s["a_proj_rs"], 1)

            def a_transposed(j, q):
                filled(act, "a", A_FREED, A_DTT, j)
                f(dtn_t[0:R, :], AW[1][0:R, :], ACT.Copy, scale=1.0).then_inc(s["a_dtnt"], 1)
                filled(act, "a", A_FREED, A_BCT, j)
                f(parts_t[:, q, :], AW[0][:, :].bitcast(BF16)[0:3 * BC, 0:GT], ACT.Copy).then_inc(s["bc_parts"], 1)

            def a_soft(j):
                positive(act, s["dt_ready"], j)
                for h in range(H):
                    filled(act, "a", A_FREED, A_DT + h, j)
                    w = AW[(A_DT + h) % 2]
                    last = f(soft[:, h, :], w[:, :], ACT.Abs, bias=dt_b[:, h:h + 1])
                    f(relu[:, h, :], w[:, :], ACT.Relu, bias=dt_b[:, h:h + 1]).then_inc(s["a_relu"], 1)
                act.wait_ge(s["a_relu"], H * (j + 1))
                link_a(j, f(soft, soft, ACT.Exp, scale=-1.0))
                f(soft, soft, ACT.Ln, bias=one[:, :]).then_inc(s["a_soft"], 1)

            def run_a(n, j, q):
                if n == 1:
                    a_rstd(j)
                if n == 3:
                    a_h(j, q)
                if n == 4:
                    a_rms(j)
                if n == 5:
                    a_xcopy(j)
                if n == 6:
                    a_silu_z(j, q)
                if n == 7:
                    a_silu_x(j, q)
                if n == 8:
                    a_proj_copy(j)
                if n == 9:
                    a_proj_rs(j)
                if n == 10:
                    a_transposed(j, q)
                if n == 11:
                    a_soft(j)

            def c_square(j):
                act.wait_ge(s["hid_ready"], j + 1)
                f(tmp_c[:, :], hid[:, :], ACT.Square).then_inc(s["c_sq"], 1)

            def c_rms(j):
                filled(act, "c", C_FREED, C_SSQ, j)
                f(rms_c[:, :], CW[1][:, :], ACT.Ln, scale=1.0 / D, bias=eps_rms[:, :]).then_inc(s["c_ln"], 1)
                act.wait_ge(s["c_ln"], j + 1)
                f(rms_c[:, :], rms_c[:, :], ACT.Exp, scale=-0.5).then_inc(s["c_rms"], 1)

            def c_act(j, use, chunk, func, done, read):
                for k in range(2):
                    filled(act, "c", C_FREED, use + k, j)
                    if chunk:
                        act.wait_ge(s[read], j * FC + chunk + k - 1)
                    f(act_c[:, k, :], CW[(use + k) % 2][:, :], func).then_inc(s[done], 1)

            def c_scale(j):
                act.wait_ge(s["c_sum"], j + 1)
                for b in range(GB):
                    last = f(act_c[:, 0, b * S:(b + 1) * S], act_c[:, 1, b * S:(b + 1) * S], ACT.Copy, scale=c_mod[:, 2, b:b + 1])
                last.then_inc(s["c_scaled"], 1)

            def c_rstd(j):
                act.wait_ge(s["c_mv"], j + 1)
                link_c(j, f(rstd_c[:, :], mv_c[:, 1, :], ACT.Ln, scale=1.0 / D, bias=eps_ln[:, :]))
                f(rstd_c[:, :], rstd_c[:, :], ACT.Exp, scale=-0.5).then_inc(s["c_rstd"], 1)

            def c_h2t(j):
                filled(act, "c", C_FREED, C_N2T, j)
                for b in range(GB):
                    last = f(h2_t[:, b * S:(b + 1) * S], CW[0][:, b * S:(b + 1) * S], ACT.Identity,
                             scale=c_mod[:, 4, b:b + 1], bias=c_mod[:, 3, b:b + 1])
                last.then_inc(s["c_h2t"], 1)

            def c_h2tok(j):
                filled(act, "c", C_FREED, C_BACK, j)
                positive(act, s["scattered"], 16 * TG * j)
                f(h2_tok[:, :, :].rearrange("p t d -> p (t d)"), CW[1][:, :], ACT.Copy).then_inc(s["c_h2tok"], 1)

            def run_c(n, j):
                if n == 3:
                    c_rms(j)
                if n == 6:
                    c_act(j, C_G01, 0, ACT.Silu, "c_silu", "c_prod")
                if n == 7:
                    c_act(j, C_G23, 2, ACT.Silu, "c_silu", "c_prod")
                if n == 10:
                    c_scale(j)
                if n == 11:
                    c_rstd(j)
                if n == 12:
                    c_h2t(j)
                    c_h2tok(j)
                if n == 13:
                    c_act(j, C_V01, 0, ACT.Gelu, "c_gelu", "c_sprod")
                if n == 14:
                    c_act(j, C_V23, 2, ACT.Gelu, "c_gelu", "c_sprod")

            def decay(g, q, n):
                if n == 0:
                    act.wait_ge(s["dt_ready"], g + 1)
                positive(act, s["h_done"], g * NS + n - RING_A + 1)
                for h in range(H):
                    last = f(da[:, n % RING_A, h, :, 1:S], dt[:, q, h, :].rearrange("p (b t) -> p b t", b=GB)[:, :, 1:S],
                             ACT.Exp, scale=neg_a[:, h, n:n + 1])
                last.then_inc(s["da_ready"], 1)

            def decays(g, q, n, has_a):
                if n in TABLE_STEPS:
                    ahead = (1, 2)
                elif n - 1 in TABLE_STEPS:
                    ahead = ()
                else:
                    ahead = (1,)
                for k in ahead:
                    if n + k < NS:
                        decay(g, q, n + k)
                    elif has_a:
                        decay(g + 1, 1 - q, n + k - NS)

            def body(g, q, has_a, has_c):
                for n in range(NS):
                    act.wait_ge(s["c_full"], g * NS + n + 1)
                    wait_hc(act, back(g, n, RING_C))
                    f(cs[:, n % RING_C, :], BCC[:, :], ACT.Copy).then_inc(s["c_copied"], 1)
                    decays(g, q, n, has_a)
                    if has_c and n == 3:
                        c_square(g - 1)
                    if has_a and n == 3:
                        run_a(n, g + 1, 1 - q)
                    if has_c:
                        run_c(n, g - 1)
                    if has_a and n != 3:
                        run_a(n, g + 1, 1 - q)
                    if n - 1 in TABLE_STEPS:
                        act.preload_act_table_set(EXP_LN)

            for n in range(NS):
                run_a(n, 0, 0)
            act.preload_act_table_set(EXP_LN)
            decay(0, 0, 0)
            groups(act, body)
            for n in range(NS):
                if n == 3:
                    c_square(G - 1)
                run_c(n, G - 1)

            def e_ext(i, r):
                act.wait_ge(s["xt_read"], 2 * i + r + 1)
                positive(act, s["up2_ps"], 2 * i + r - 1)
                f(ext[:, r, :], bank[0][:, 0:P], ACT.Copy).then_inc(s["ext"], 1)

            def e_gelu(i, r):
                act.wait_ge(s["up1_ps"], 2 * i + r + 1)
                positive(act, s["prod_done"], 2 * i + r - 1)
                f(gel[:, r, :], bank[3 + r][:, :], ACT.Gelu).then_inc(s["gelu_done"], 1)

            e_ext(0, 0)
            e_ext(0, 1)
            e_gelu(0, 0)
            with act.Fori(0, TILES // 2 - 1) as i:
                e_ext(i + 1, 0)
                e_gelu(i, 1)
                e_ext(i + 1, 1)
                e_gelu(i + 1, 0)
            e_gelu(TILES // 2 - 1, 1)

        @block.vector
        def _(dve):
            count = [0]

            def setup(ins):
                count[0] += 1
                ins.then_inc(s["dve_setup"], 1)
                dve.wait_ge(s["dve_setup"], count[0])

            def sign_and_floor(dst, src, t1, t2):
                setup(dve.tensor_scalar(t1, src, 0.0, 2.0, ALU.is_ge, ALU.mult))
                setup(dve.tensor_scalar(t1, t1, -1.0, None, ALU.add))
                setup(dve.tensor_tensor(t2, src, t1, ALU.mult))
                setup(dve.tensor_scalar(t2, t2, 0.25, None, ALU.max))
                setup(dve.tensor_tensor(dst, t1, t2, ALU.mult))

            setup(dve.memset(da[:, :, :, :, :], 0.0))
            setup(dve.memset(xpad[:, :, :, 0:K - 1], 0.0))
            dve.wait_ge(s["mod_ps"], 1)
            setup(dve.tensor_copy(mods[:, :, :], Y[0][:, 0:6 * B].rearrange("p (m b) -> p m b", m=6)))
            setup(dve.tensor_copy(gate_t1[:, :], Y[0][0:B, P:P + D]))
            sign_and_floor(gate16[:, :], gate_t1[:, :], gate_t3[:, :], gate_t2[:, :])
            for m in (1, 4):
                setup(dve.tensor_scalar(mods[:, m, :], mods[:, m, :], 1.0, None, ALU.add))
            sign_and_floor(mods[:, 2, :], mods[:, 2, :], mod_t1[:, :], mod_t2[:, :])
            dve.wait_ge(s["weights_in"], WEIGHTS)
            setup(dve.tensor_scalar(w_dt[:, :], w_dt[:, :], ln_dt[:, :], None, ALU.mult))
            dve.wait_ge(s["exp_a"], 1)
            setup(dve.tensor_scalar(neg_a[:, :, :], neg_a[:, :, :], -1.0, None, ALU.mult))
            assert count[0] == DVE_SETUP
            for r in range(B // 4):
                dve.wait_ge(s["gate_ps"], r + 1)
                dve.tensor_copy(gate_b[:, 4 * r:4 * r + 4, :].rearrange("p b d -> p (b d)"), Y[(r + 1) % 2][:, :])\
                    .then_inc(s["gate_read"], 1)

            link_a = chained(dve, "a_dve", A_LINKS)
            link_c = chained(dve, "c_dve", C_LINKS)

            def aggregate(j, stats, mv, link, done):
                even, odd = (stats[:, :, k:k + 3].rearrange("p t k -> p k t") for k in (0, 3))
                dve.tensor_tensor(mv[:, 0, :], even[:, 1], odd[:, 1], ALU.add)
                dve.tensor_tensor(mv[:, 1, :], even[:, 2], odd[:, 2], ALU.add)
                link(j, dve.tensor_tensor(mv[:, 2, :], even[:, 1], odd[:, 1], ALU.subtract))
                dve.tensor_scalar(mv[:, 0, :], mv[:, 0, :], 0.5, None, ALU.mult)
                link(j, dve.tensor_tensor(mv[:, 2, :], mv[:, 2, :], mv[:, 2, :], ALU.mult))
                dve.scalar_tensor_tensor(mv[:, 1, :], mv[:, 2, :], D / 4.0, mv[:, 1, :], ALU.mult, ALU.add).then_inc(s[done], 1)

            def a_stats(j):
                if isinstance(j, int) and j == 0:
                    dve.wait_ge(s["x_first_in"], 16)
                else:
                    dve.wait_ge(s["x_rest_in"], 16 * (G - 1))
                    dve.wait_ge(s["a_h"], j)
                dve.tensor_copy(a_mod[:, :, :], mods[:, 0:2, bass.ds(GB * j, GB)])
                for t in range(TG):
                    last = dve.bn_stats(stats_a[:, t, :], x_all[:, bass.ds(j * TG + t, 1), :].rearrange("p o d -> p (o d)"))
                link_a(j, last)
                aggregate(j, stats_a, mv_a, link_a, "a_mv")

            def a_norm(j):
                dve.wait_ge(s["a_rstd"], j + 1)
                dve.wait_ge(s["a_mv"], j + 1)
                for t in range(TG):
                    last = dve.tensor_scalar(xn[:, t, :], x_all[:, bass.ds(j * TG + t, 1), :].rearrange("p o d -> p (o d)"),
                                             mv_a[:, 0, t:t + 1], rstd_a[:, t:t + 1], ALU.subtract, ALU.mult)
                last.then_inc(s["a_xn"], 1)

            def a_hn(j, q):
                dve.wait_ge(s["a_rms"], j + 1)
                dve.scalar_tensor_tensor(hn, h_t[:, q, :], ln_in[:, :], rms_a, ALU.mult, ALU.mult).then_inc(s["a_hn"], 1)

            def a_conv(j, taps):
                for k in taps:
                    if k == 0:
                        positive(dve, s["a_silu"], j)
                        for h in range(H):
                            dve.wait_ge(s["a_xpad"], H * j + h + 1)
                            last = dve.tensor_scalar(conv[:, h], xpad[:, h, :, K - 1:PAD], conv_w[:, h, K - 1:K],
                                                     conv_b[:, h:h + 1], ALU.mult, ALU.add)
                    else:
                        for h in range(H):
                            last = dve.scalar_tensor_tensor(conv[:, h], xpad[:, h, :, k - 1:k - 1 + S],
                                                            conv_w[:, h, k - 1:k], conv[:, h], ALU.mult, ALU.add)
                    if k < K - 1:
                        link_a(j, last)
                    else:
                        last.then_inc(s["a_conv"], 1)

            def a_ms(j):
                dve.wait_ge(s["a_proj_copy"], j + 1)
                dve.tensor_reduce(proj_ms[:, 0, :], proj_sq[:, :, 0:R], AX, ALU.add)
                dve.tensor_reduce(proj_ms[:, 1:3, :].rearrange("p s t -> p t s"),
                                  proj_sq[:, :, R:XP].rearrange("p t (s n) -> p t s n", s=2), AX, ALU.add)\
                    .then_inc(s["a_proj_ms"], 1)

            def a_parts(j):
                dve.wait_ge(s["a_proj_rs"], j + 1)
                dve.tensor_tensor(dtn, proj[:, :, 0:R], proj_rs[:, 0, :].unsqueeze(2).broadcast_to([P, TG, R]), ALU.mult)\
                    .then_inc(s["a_dtn"], 1)
                b4 = bcn.rearrange("p t (s n) -> p t s n", s=2)
                link_a(j, dve.tensor_tensor(b4, proj[:, :, R:XP].rearrange("p t (s n) -> p t s n", s=2),
                                            proj_rs[:, 1:3, :].rearrange("p s t -> p t s").unsqueeze(3)
                                            .broadcast_to([P, TG, 2, NS]), ALU.mult))
                link_a(j, dve.tensor_tensor(bcn, bcn, ln_bc[:, :].unsqueeze(1).broadcast_to([P, TG, BC]), ALU.mult))
                for k in range(2):
                    piece = parts_tok[:, :, k * BC:(k + 1) * BC]
                    link_a(j, dve.tensor_copy(piece, bcn))
                    link_a(j, dve.tensor_tensor(bcn, bcn, piece, ALU.subtract))
                dve.tensor_copy(parts_tok[:, :, 2 * BC:3 * BC], bcn).then_inc(s["a_parts"], 1)

            def a_u(j, q):
                dve.wait_ge(s["a_soft"], j + 1)
                dve.tensor_tensor(dt[:, q], soft, relu, ALU.add).then_inc(s["dt_ready"], 1)
                dve.wait_ge(s["dt_ready"], j + 1)
                dve.tensor_tensor(u[:, q], dt[:, q], xs_[:, q], ALU.mult).then_inc(s["u_ready"], 1)

            def run_a(n, j, q):
                if n == 0:
                    a_stats(j)
                if n == 1:
                    a_norm(j)
                if n == 4:
                    a_hn(j, q)
                if n == 5:
                    a_conv(j, (0, 1))
                if n == 6:
                    a_conv(j, (2, 3))
                if n == 8:
                    a_ms(j)
                if n == 9:
                    a_parts(j)
                if n == 12:
                    a_u(j, q)

            def c_y(j, q):
                dve.wait_ge(s["nsum_done"], (j + 1) * NS)
                dve.tensor_copy(c_mod[:, :, :], mods[:, :, bass.ds(GB * j, GB)])
                for h in range(H):
                    last = dve.scalar_tensor_tensor(yt[:, h, :], xs_[:, q, h, :], d_skip[:, h:h + 1], Y[h][:, :], ALU.mult, ALU.add)
                last.then_inc(s["y_read"], 1)
                dve.wait_ge(s["y_read"], j + 1)
                dve.tensor_tensor(yt, yt, zs[:, q], ALU.mult).then_inc(s["yg_ready"], 1)

            def c_hid(j, q):
                filled(dve, "c", C_FREED, C_OUT, j)
                dve.tensor_tensor(hid[:, :], CW[0][:, :], h_t[:, q, :], ALU.add).then_inc(s["hid_ready"], 1)

            def c_hn(j):
                dve.wait_ge(s["c_rms"], j + 1)
                dve.scalar_tensor_tensor(tmp_c[:, :], hid[:, :], ln_moe[:, :], rms_c[:, :], ALU.mult, ALU.mult)\
                    .then_inc(s["c_hn"], 1)

            def c_product(j, use, chunk, acted, done):
                for k in range(2):
                    dve.wait_ge(s[acted], j * FC + chunk + k + 1)
                    filled(dve, "c", C_FREED, use + k, j)
                    dve.tensor_tensor(prod_c[:, chunk + k, :], act_c[:, k, :], CW[(use + k) % 2][:, :], ALU.mult)\
                        .then_inc(s[done], 1)

            def c_sum(j):
                filled(dve, "c", C_FREED, C_DOWN, j)
                dve.tensor_tensor(act_c[:, 1, :], CW[0][:, :], hid[:, :], ALU.add).then_inc(s["c_sum"], 1)

            def group_of(j):
                return x_all[:, bass.ds(j * TG, TG), :]

            def c_x2(j):
                filled(dve, "c", C_FREED, C_OGT, j)
                dve.tensor_tensor(group_of(j), CW[1][:, :].rearrange("p (t d) -> p t d", t=TG), group_of(j), ALU.add)\
                    .then_inc(s["x2_ready"], 1)
                apart(dve)
                dve.wait_ge(s["x2_ready"], j + 1)
                for t in range(TG):
                    last = dve.bn_stats(stats_c[:, t, :], x_all[:, bass.ds(j * TG + t, 1), :].rearrange("p o d -> p (o d)"))
                link_c(j, last)
                aggregate(j, stats_c, mv_c, link_c, "c_mv")

            def c_n2(j):
                dve.wait_ge(s["c_rstd"], j + 1)
                dve.wait_ge(s["c_mv"], j + 1)
                for t in range(TG):
                    last = dve.tensor_scalar(n2[:, t, :], x_all[:, bass.ds(j * TG + t, 1), :].rearrange("p o d -> p (o d)"),
                                             mv_c[:, 0, t:t + 1], rstd_c[:, t:t + 1], ALU.subtract, ALU.mult)
                last.then_inc(s["c_n2"], 1)

            def over_e(a):
                return a.unsqueeze(2).broadcast_to([P, TG, NE])

            def c_onehot(j):
                filled(dve, "c", C_FREED, C_LOGIT, j)
                lg = CW[0][:, 0:TG * NE].rearrange("p (t e) -> p t e", t=TG)
                link_c(j, dve.tensor_reduce(lmax[:, :], lg, AX, ALU.max))
                dve.tensor_tensor(eq[:, :, :], lg, over_e(lmax[:, :]), ALU.is_equal).then_inc(s["c_eq"], 1)
                dve.wait_ge(s["c_eq"], j + 1)
                link_c(j, dve.tensor_tensor(eq[:, :, :], eq[:, :, :], rev[:, :].unsqueeze(1).broadcast_to([P, TG, NE]), ALU.mult))
                link_c(j, dve.tensor_reduce(emax[:, :], eq[:, :, :], AX, ALU.max))
                dve.tensor_tensor(onehot[:, :, :], eq[:, :, :], over_e(emax[:, :]), ALU.is_equal).then_inc(s["c_onehot"], 1)
                dve.wait_ge(s["c_onehot"], j + 1)
                link_c(j, dve.tensor_copy(onehot_all[:, bass.ds(j * TG, TG), :], onehot[:, :, :]))

            def c_slots(j):
                filled(dve, "c", C_FREED, C_RANK, j)
                w = CW[1][:, 0:2 * TG * NE].rearrange("p (k t e) -> p k t e", k=2, t=TG)
                link_c(j, dve.tensor_copy(base5[:, 0, :], base5[:, TG, :]))
                for t in range(TG):
                    link_c(j, dve.tensor_tensor(base5[:, t + 1, :], base5[:, t, :], w[:, 1, t, :], ALU.add))
                dve.tensor_tensor(rk[:, :, :], w[:, 0], base5[:, 0:TG, :], ALU.add).then_inc(s["c_counts"], 1)
                dve.wait_ge(s["c_counts"], j + 1)
                link_c(j, dve.tensor_tensor(rk[:, :, :], rk[:, :, :], onehot[:, :, :], ALU.mult))
                link_c(j, dve.tensor_reduce(rank[:, :], rk[:, :, :], AX, ALU.add))
                dve.tensor_copy(rank_all[:, bass.ds(j * TG, TG)], rank[:, :])
                link_c(j, dve.tensor_scalar(slot_f[:, :], emax[:, :], -float(REG), float(NE * REG), ALU.mult, ALU.add))
                link_c(j, dve.tensor_tensor(slot_f[:, :], slot_f[:, :], rank[:, :], ALU.add))
                positive(dve, s["scattered"], 16 * TG * j)
                dve.tensor_copy(slot[:, :], slot_f[:, :]).then_inc(s["c_slot"], 1)

            def c_base(j):
                filled(dve, "c", C_FREED, C_SHARED, j)
                g4 = gate_b[:, bass.ds(GB * j, GB), :].unsqueeze(2).broadcast_to([P, GB, TG // GB, D])
                dve.tensor_tensor(rms_c[:, :].rearrange("p (b t d) -> p b t d", b=GB, d=D),
                                  CW[0][:, :].rearrange("p (b t d) -> p b t d", b=GB, d=D), g4, ALU.mult).then_inc(s["c_gated"], 1)
                dve.wait_ge(s["c_gated"], j + 1)
                dve.tensor_tensor(group_of(j), rms_c[:, :].rearrange("p (t d) -> p t d", t=TG), group_of(j), ALU.add)\
                    .then_inc(s["base_ready"], 1)

            def run_c(n, j, q):
                if n == 1:
                    c_y(j, q)
                if n == 2:
                    c_hid(j, q)
                if n == 4:
                    c_hn(j)
                if n == 6:
                    c_product(j, C_U01, 0, "c_silu", "c_prod")
                if n == 8:
                    c_product(j, C_U23, 2, "c_silu", "c_prod")
                if n == 9:
                    c_sum(j)
                if n == 10:
                    c_x2(j)
                if n == 11:
                    c_n2(j)
                if n == 12:
                    c_onehot(j)
                if n == 13:
                    c_product(j, C_W01, 0, "c_gelu", "c_sprod")
                if n == 14:
                    c_product(j, C_W23, 2, "c_gelu", "c_sprod")
                if n == 15:
                    c_slots(j)
                    c_base(j)

            def scan_input(g, q, n):
                if n == 0:
                    dve.wait_ge(s["u_ready"], g + 1)
                dve.wait_ge(s["b_full"], g * NS + n + 1)
                positive(dve, s["h_done"], g * NS + n - RING_X + 1)
                dve.tensor_tensor(bx[:, n % RING_X], u[:, q], BB[:, :].unsqueeze(1).broadcast_to([P, H, GT]), ALU.mult)\
                    .then_inc(s["bx_done"], 1)

            def product(g, n):
                if n in POOL_N:
                    return
                dve.wait_ge(s["c_copied"], g * NS + n + 1)
                dve.wait_ge(s["h_done"], g * NS + n + 1)
                positive(dve, s["nsum_done"], g * NS + n - RING_P + 1)
                dve.tensor_tensor(hc[:, n % RING_P], hs[:, n % RING_H],
                                  cs[:, n % RING_C].unsqueeze(1).broadcast_to([P, H, GT]), ALU.mult)\
                    .then_inc(s["hc_dve"], 1)

            def body(g, q, has_a, has_c):
                for n in range(NS):
                    if n + 1 < NS:
                        scan_input(g, q, n + 1)
                    elif has_a:
                        scan_input(g + 1, 1 - q, 0)
                    dve.wait_ge(s["bx_done"], g * NS + n + 1)
                    dve.wait_ge(s["da_ready"], g * NS + n + 1)
                    wait_hc(dve, back(g, n, RING_H))
                    dve.tensor_tensor_scan(hs[:, n % RING_H].rearrange("p h t -> p (h t)"),
                                           da[:, n % RING_A].rearrange("p h b t -> p (h b t)"),
                                           bx[:, n % RING_X].rearrange("p h t -> p (h t)"), 0.0, ALU.mult, ALU.add)\
                        .then_inc(s["h_done"], 1)
                    step = back(g, n, 1)
                    if step is not None:
                        product(*step)
                    if has_a:
                        run_a(n, g + 1, 1 - q)
                    if has_c:
                        run_c(n, g - 1, 1 - q)

            for n in range(NS):
                run_a(n, 0, 0)
            scan_input(0, 0, 0)
            groups(dve, body)
            product(G - 1, NS - 1)
            for n in range(NS):
                run_c(n, G - 1, (G - 1) % 2)

            link_e = chained(dve, "e_dve", 10 ** 6)
            link = lambda ins: link_e(0, ins)
            tt = dve.tensor_tensor
            counts = base5[:, TG, :]
            link(tt(tail_f[:, :], counts, region[:, :], ALU.add))
            link(dve.tensor_scalar(tail_f[:, :], tail_f[:, :], pid[:, :], None, ALU.add))
            dve.tensor_copy(tail[:, :], tail_f[:, :]).then_inc(s["tail_idx"], 1)
            k_big = big[:, 0:NT, :]
            link(tt(k_big, counts.unsqueeze(1).broadcast_to([P, NT, NE]), iota_k[:, :].unsqueeze(2).broadcast_to([P, NT, NE]), ALU.is_gt))
            link(dve.tensor_reduce(n_tiles[:, :], k_big.rearrange("p k e -> p e k"), AX, ALU.add))
            link(dve.tensor_tensor_scan(last_tile[:, :], ones8[:, :], n_tiles[:, :], 0.0, ALU.mult, ALU.add))
            link(tt(first_tile[:, :], last_tile[:, :], n_tiles[:, :], ALU.subtract))
            each = [P, TILES, NE]
            link(tt(big[:, :, :], iota_j[:, :].unsqueeze(2).broadcast_to(each), last_tile[:, :].unsqueeze(1).broadcast_to(each), ALU.is_ge))
            link(dve.tensor_reduce(ej[:, :], big[:, :, :], AX, ALU.add))
            link(tt(big[:, :, :], big[:, :, :], n_tiles[:, :].unsqueeze(1).broadcast_to(each), ALU.mult))
            link(dve.tensor_reduce(kj[:, :], big[:, :, :], AX, ALU.add))
            link(tt(kj[:, :], iota_j[:, :], kj[:, :], ALU.subtract))
            link(dve.tensor_scalar(vj[:, :], ej[:, :], float(NE), float(P), ALU.is_lt, ALU.mult))
            link(tt(kj[:, :], kj[:, :], vj[:, :], ALU.mult))
            link(dve.scalar_tensor_tensor(rowf[:, :], ej[:, :], float(REG), kj[:, :], ALU.mult, ALU.add))
            link(dve.tensor_scalar(ej[:, :], ej[:, :], float(NE - 1), None, ALU.min))
            dve.tensor_copy(row_tab[:, :], rowf[:, :])
            dve.tensor_copy(exp_tab[:, :], ej[:, :]).then_inc(s["tables"], 1)
            each = [P, NT, NE]
            link(tt(k_big, onehot_all[:, :, :], first_tile[:, :].unsqueeze(1).broadcast_to(each), ALU.mult))
            link(dve.tensor_reduce(gidx_f[:, :], k_big, AX, ALU.add))
            link(dve.scalar_tensor_tensor(gidx_f[:, :], gidx_f[:, :], float(P), rank_all[:, :], ALU.mult, ALU.add))
            dve.tensor_copy(gidx[:, :], gidx_f[:, :]).then_inc(s["gather_idx"], 1)

            def e_product(i, r):
                dve.wait_ge(s["gelu_done"], 2 * i + r + 1)
                dve.wait_ge(s["up2_ps"], 2 * i + r + 1)
                positive(dve, s["prodt_ps"], 2 * i + r - 1)
                tt(pe_[:, r, :], gel[:, r, :], bank[5 + r][:, :], ALU.mult).then_inc(s["prod_done"], 1)

            def e_prod_t(i, r):
                dve.wait_ge(s["prodt_ps"], 2 * i + r + 1)
                dve.tensor_copy(pet[:, r, :], bank[1][:, :]).then_inc(s["prodt"], 1)

            def e_out(i, r):
                dve.wait_ge(s["down_ps"], 2 * i + r + 1)
                positive(dve, s[f"ys_out{r}"], 16 * i)
                dve.tensor_copy(yo[:, r, :], bank[2][:, 0:D]).then_inc(s["yo"], 1)

            e_product(0, 0)
            with dve.Fori(0, TILES // 2 - 1) as i:
                e_prod_t(i, 0)
                e_product(i, 1)
                e_out(i, 0)
                e_prod_t(i, 1)
                e_product(i + 1, 0)
                e_out(i, 1)
            L = TILES // 2 - 1
            e_prod_t(L, 0)
            e_product(L, 1)
            e_out(L, 0)
            e_prod_t(L, 1)
            e_out(L, 1)

            for j in range(G):
                rows = y_rows[:, j * TG:(j + 1) * TG, :]
                dve.wait_ge(s[f"gathered{j}"], 16 * TG)
                g4 = gate_b[:, GB * j:GB * (j + 1), :].unsqueeze(2).broadcast_to([P, GB, TG // GB, D])
                tt(rows.rearrange("p (b t) d -> p b t d", b=GB), rows.rearrange("p (b t) d -> p b t d", b=GB), g4, ALU.mult)\
                    .then_inc(s["weighted"], 1)
                dve.wait_ge(s["weighted"], j + 1)
                tt(x_all[:, j * TG:(j + 1) * TG, :], x_all[:, j * TG:(j + 1) * TG, :], rows, ALU.add).then_inc(s["final_sum"], 1)


_INS = ["L0_attn_hidden_states", "L0_attn_in_proj_w", "L0_attn_conv_w", "L0_attn_conv_b", "L0_attn_x_proj_w",
        "L0_attn_dt_proj_w", "L0_attn_dt_proj_b", "L0_attn_dt_ln_w", "L0_attn_b_ln_w", "L0_attn_c_ln_w", "L0_attn_A_log",
        "L0_attn_D_skip", "L0_attn_out_proj_w", "L0_attn_input_ln_w", "L0_attn_pre_moe_ln_w", "L0_attn_gate_w",
        "L0_attn_up_w", "L0_attn_down_w", "L0_ffn_w1s", "L0_ffn_w2s", "L0_ffn_w3s", "L0_ffn_W1", "L0_ffn_W2", "L0_ffn_W3",
        "L0_ffn_Wg", "L0_c", "L0_wmod"]

_BY_HALF = ("L0_attn_conv_b", "L0_attn_dt_proj_b", "L0_attn_D_skip")


def kernel(**inputs):
    import numpy as _np
    import concourse.bacc as _bacc
    from concourse import mybir as _mybir
    from concourse.bass_utils import run_bass_kernel_spmd as _run

    nc = _bacc.Bacc("TRN2", target_bir_lowering=False, num_devices=1)
    arrays, io = {}, {}
    for name in _INS:
        a = _np.asarray(inputs[name])
        if name in _BY_HALF:
            a = a.reshape(H, P).T
        a = _np.ascontiguousarray(a)
        arrays[f"in_{name}"] = a
        io[name] = nc.dram_tensor(f"in_{name}", a.shape, _mybir.dt.from_np(a.dtype), kind="ExternalInput").ap()
    out = nc.dram_tensor("out_0", (B, S, D), _mybir.dt.float32, kind="ExternalOutput").ap()
    build(nc, io, out)
    r = _run(nc, [arrays], core_ids=[0])
    return r.results[0]["out_0"]
```

```python
from contextlib import ExitStack

import numpy as np
import concourse.bass as bass
from concourse import mybir

F32 = mybir.dt.float32
BF16 = mybir.dt.bfloat16
U32 = mybir.dt.uint32
I32 = mybir.dt.int32
ALU = mybir.AluOpType
ACT = mybir.ActivationFunctionType
AX = mybir.AxisListType.X

P = 128
B, S, D = 16, 256, 128
DI, NS, R, K = 256, 16, 64, 4
FF = 512
NE = 8
GB = 2
G = B // GB
GT = GB * S
TG = GT // P
NT = B * S // P
H = DI // P
FC = FF // P
XP = R + 2 * NS
BC = 2 * NS
REG = B * S + P
SPARE = NE * REG
TILES = NT + NE
U = 4
EPS_LN, EPS_RMS = 1e-5, 1e-6

RING_A, RING_X, RING_H, RING_C, RING_P = 4, 2, 2, 4, 2
POOL_N = (0, 4, 5, 8, 10, 12, 15)


WEIGHTS = 16 * 21
POOL_SETUP, DVE_SETUP = 27, 20
GATE_ROWS = 9
A_LINKS, C_LINKS = 11, 15
EXP_LN = "natural_log_exp_and_others"


def positive(eng, sem, value):
    if not (isinstance(value, int) and value <= 0):
        eng.wait_ge(sem, value)


def build(nc, io, out):
    ctx = ExitStack()
    with ctx:
        def sb(name, shape, dt=F32):
            return ctx.enter_context(nc.sbuf_tensor(name, shape, dt))

        names = (
            "x_first_in", "x_rest_in", "cond_in", "weights_in", "experts_in", "late_experts_in",
            "pool_setup", "dve_setup", "zeros_out", "silu_c", "silu_ct_ps", "silu_ct", "mod_ps",
            "gate_ps", "gate_read", "exp_a",
            "a0_full", "a1_full", "c0_full", "c1_full",
            "a_dve", "a_act", "a_mv", "a_rstd", "a_shift", "a_xn", "a_h", "a_sq", "a_ln", "a_rms", "a_hn", "a_xpad", "a_conv",
            "a_zs", "a_silu", "a_proj_copy", "a_proj_ms", "a_proj_rs", "a_dtn", "a_parts", "a_dtnt", "bc_parts",
            "a_relu", "a_soft", "dt_ready", "u_ready",
            "b_full", "c_rows_out", *(f"c_in{r}" for r in range(RING_C)), "da_ready", "bx_done", "h_done", "hc_dve", "hc_pool", "nsum_done",
            "c_dve", "c_act", "yg_ready", "hid_ready", "c_sq", "c_ln", "c_rms", "c_hn", "c_silu", "c_prod",
            "c_scaled", "x2_ready", "c_mv", "c_rstd", "c_shift", "c_n2", "c_h2t", "c_h2tok", "c_eq", "c_onehot",
            "c_counts", "c_ranked", "c_slot", "scattered", "c_gelu", "c_sprod", "c_gated", "base_ready",
            "e_dve", "tail_idx", "tails_out", "tables", *(f"xt_in{r}" for r in range(U)), "xt_read", "ext", "up1_ps", "up2_ps",
            "gelu_done", "prod_done", "prodt_ps", "prodt", "down_ps", "yo", "numbered", "row_idx", "ys_out0", "ys_out1",
            *(f"gathered{j}" for j in range(G)), "weighted", "final_sum", "out_done",
        )
        s = {n: ctx.enter_context(nc.semaphore(n)) for n in names}

        x_all = sb("x_all", [P, NT, D])
        gate_b = sb("gate_b", [P, B, D])
        w_in = sb("w_in", [P, 2 * DI])
        w_xp = sb("w_xp", [P, H, XP])
        w_dt = sb("w_dt", [R, DI])
        w_out = sb("w_out", [P, H, D])
        w_gate, w_up = sb("w_gate", [P, FF]), sb("w_up", [P, FF])
        w_down = sb("w_down", [P, FC, D])
        w1s, w2s = sb("w1s", [P, FF]), sb("w2s", [P, FF])
        w3s = sb("w3s", [P, FC, D])
        w_route = sb("w_route", [P, NE])
        e_w1 = sb("e_w1", [P, NE, FF])
        sel = sb("sel", [3 * NS, NS], BF16)
        ident, ones = sb("ident", [P, P]), sb("ones", [P, P])
        identb, onesb, tri = sb("identb", [P, P], BF16), sb("onesb", [P, P], BF16), sb("tri", [P, P], BF16)
        mods = sb("mods", [P, 6, B])
        neg_a = sb("neg_a", [P, H, NS])
        conv_w, conv_b = sb("conv_w", [P, H, K]), sb("conv_b", [P, H])
        dt_b, d_skip, d_diag = sb("dt_b", [P, H]), sb("d_skip", [P, H]), sb("d_diag", [P, H, P])
        ln_in, ln_moe, ln_dt = sb("ln_in", [P, 1]), sb("ln_moe", [P, 1]), sb("ln_dt", [R, 1])
        ln_bc = sb("ln_bc", [P, BC])
        eps_ln, eps_rms, one = sb("eps_ln", [P, 1]), sb("eps_rms", [P, 1]), sb("one", [P, 1])
        c_sb, c_silu, c_t = sb("c_sb", [B, D]), sb("c_silu_sb", [B, D]), sb("c_t", [P, B])
        gate16 = sb("gate16", [B, D])

        SHARED = 2 * NE * FF
        shared = sb("a_or_experts", [P, SHARED])
        e_w2 = shared[:, 0:NE * FF].rearrange("p (e f) -> p e f", e=NE)
        e_w3 = shared[:, NE * FF:2 * NE * FF].rearrange("p (e c d) -> p e c d", e=NE, c=FC)
        taken = [0]

        def part(n):
            taken[0] += n
            assert taken[0] <= SHARED
            return shared[:, taken[0] - n:taken[0]]

        xn = part(GT).rearrange("p (t d) -> p t d", t=TG)
        sq_a, rms_a, hn = part(GT), part(GT), part(GT)
        PAD = K - 1 + S
        xpad = part(H * GB * PAD).rearrange("p (h b t) -> p h b t", h=H, b=GB)
        conv = part(H * GT).rearrange("p (h b t) -> p h b t", h=H, b=GB)
        proj_sq = part(TG * XP).rearrange("p (t c) -> p t c", t=TG)
        proj = part(TG * XP).rearrange("p (t c) -> p t c", t=TG)
        dtc = part(TG * (R + NS)).rearrange("p (t c) -> p t c", t=TG)
        dtn_t = part(GT)
        bcn = part(TG * BC).rearrange("p (t c) -> p t c", t=TG)
        soft = part(H * GT).rearrange("p (h t) -> p h t", h=H)
        relu = part(H * GT).rearrange("p (h t) -> p h t", h=H)

        parts_tok = sb("parts_tok", [P, TG, 3 * NS], BF16)
        a_mod, stats_a, mv_a = sb("a_mod_sb", [P, 2, GB]), sb("stats_a", [P, TG, 6]), sb("mv_a", [P, 3, TG])
        rstd_a, proj_ms, proj_rs = sb("rstd_a", [P, TG]), sb("proj_ms", [P, 3, TG]), sb("proj_rs", [P, 3, TG])
        h_t = sb("h_t", [P, 2, GT])
        parts_t = sb("parts_t", [3 * NS, 2, GT], BF16)
        dt = sb("dt", [P, 2, H, GT])
        NKEEP = 2 * H * GT
        keep = sb("keep", [P, 3 * NKEEP])
        u = keep[:, 0:NKEEP].rearrange("p (q h t) -> p q h t", q=2, h=H)
        xs_ = keep[:, NKEEP:2 * NKEEP].rearrange("p (q h t) -> p q h t", q=2, h=H)
        zs = keep[:, 2 * NKEEP:3 * NKEEP].rearrange("p (q h t) -> p q h t", q=2, h=H)
        y_rows = keep[:, 0:NT * D].rearrange("p (t d) -> p t d", t=NT)

        da = sb("da", [P, RING_A, H, GB, S])
        bx = sb("bx", [P, RING_X, H, GT])
        hs = sb("hs", [P, RING_H, H, GT])
        cs = sb("cs", [P, RING_C, GT])
        hc = sb("hc", [P, RING_P, H, GT])

        c_mod = sb("c_mod_sb", [P, 6, GB])
        hid, tmp_c, rms_c = sb("hid", [P, GT]), sb("tmp_c", [P, GT]), sb("rms_c", [P, GT])
        act_c = sb("act_c", [P, 2, GT])
        gate_t1, gate_t2, gate_t3 = (hid[0:B, k * D:(k + 1) * D] for k in range(3))
        mod_t1, mod_t2 = tmp_c[:, 0:B], tmp_c[:, B:2 * B]
        prod_c = sb("prod_c", [P, FC, GT])
        yt = prod_c[:, 0:H, :]
        wmod = prod_c[:, :, :].rearrange("p c t -> p (c t)")[:, 0:6 * D]
        n2 = tmp_c[:, :].rearrange("p (t d) -> p t d", t=TG)
        h2_t, h2_tok = sb("h2_t", [P, GT]), sb("h2_tok", [P, TG, D + 1])
        stats_c, mv_c, rstd_c = sb("stats_c", [P, TG, 6]), sb("mv_c", [P, 3, TG]), sb("rstd_c", [P, TG])
        lmax, eq, rev = sb("lmax", [P, TG]), sb("eq", [P, TG, NE]), sb("rev", [P, NE])
        emax, onehot = sb("emax", [P, TG]), sb("onehot", [P, TG, NE], BF16)
        base5, rk, rank = sb("base5", [P, TG + 1, NE]), sb("rk", [P, TG, NE]), sb("rank", [P, TG])
        counted = sb("counted", [P, 2, TG, NE])
        slot_f, slot = sb("slot_f", [P, TG]), sb("slot", [P, TG], U32)

        NUMBERS = NT + 2 * NE
        iota_k, iota_j, token = (sb(n, [P, NUMBERS]) for n in ("iota_k", "iota_j", "token"))
        iota_i = sb("iota_i", [P, NUMBERS], I32)
        region, pid = sb("region", [P, NE]), sb("pid", [P, 1])
        big = sb("big", [P, TILES, NE])
        n_tiles, last_tile = sb("n_tiles", [P, NE]), sb("last_tile", [P, NE])
        ones8 = sb("ones8", [P, NE])
        ej, kj, rowf = sb("ej", [P, TILES]), sb("kj", [P, TILES]), sb("rowf", [P, TILES])
        row_tab, exp_tab = sb("row_tab", [P, TILES], I32), sb("exp_tab", [P, TILES], I32)
        tail_f, tail = sb("tail_f", [P, NE]), sb("tail", [P, NE], U32)
        number, row_idx = sb("number", [P, TILES]), sb("row_idx", [P, 2], U32)

        blank = hc[:, :, :, :].rearrange("p r h t -> p (r h t)")[:, 0:NE * (D + 1)].rearrange("p (e d) -> p e d", e=NE)

        ring = hs[:, :, :, :].rearrange("p r h t -> p (r h t)")
        ext = ring[:, 0:2 * P].rearrange("p (r d) -> p r d", r=2)
        yo = ring[:, 2 * P:4 * P].rearrange("p (r d) -> p r d", r=2)
        xt = ring[:, 4 * P:4 * P + U * (D + 1)].rearrange("p (r d) -> p r d", r=U)
        ring2 = da[:, :, :, :, :].rearrange("p r h b t -> p (r h b t)")
        gel = ring2[:, 0:2 * FF].rearrange("p (r f) -> p r f", r=2)
        pe_ = ring2[:, 2 * FF:4 * FF].rearrange("p (r f) -> p r f", r=2)
        pet = ring2[:, 4 * FF:6 * FF].rearrange("p (r f) -> p r f", r=2)

        bank = [ctx.enter_context(nc.psum_tensor(f"bank{i}", [P, 512], F32)) for i in range(8)]
        BB, Y, AW, CW = bank[0:2], bank[2:4], bank[4:6], bank[6:8]

        xs_rows = nc.dram_tensor("xs_rows", (SPARE + NE * P, D + 1), F32, kind="Internal").ap()
        ys_rows = nc.dram_tensor("ys_rows", (NUMBERS * P, D), F32, kind="Internal").ap()

        c_rows = nc.dram_tensor("c_rows", (2, NS, GT), F32, kind="Internal").ap()

        A_FREED = [("a_h", 1, 1), ("a_ln", 1, 1), ("a_xpad", 2, 1), ("a_xpad", 2, 2), ("a_zs", 2, 1), ("a_zs", 2, 2),
                   ("a_proj_copy", 1, 1), ("a_dtnt", 1, 1), ("bc_parts", 1, 1), ("a_relu", 2, 1), ("a_relu", 2, 2)]
        C_FREED = [("c_sq", 1, 1), ("c_ln", 1, 1)]
        for k in range(1, FC + 1):
            C_FREED += [("c_silu", FC, k), ("c_prod", FC, k)]
        C_FREED += [("c_scaled", 1, 1), ("x2_ready", 1, 1), ("c_h2t", 1, 1), ("c_h2tok", 1, 1), ("c_eq", 1, 1),
                    ("c_counts", 1, 1)]
        for k in range(1, FC + 1):
            C_FREED += [("c_gelu", FC, k), ("c_sprod", FC, k)]
        C_FREED += [("c_gated", 1, 1)]

        def take(pe, uses, i, j):
            if i < 2:
                i, j = max(k for k in range(len(uses)) if k % 2 == i % 2) , j - 1
            else:
                i -= 2
            name, per, count = uses[i]
            positive(pe, s[name], j * per + count)

        def filled(eng, chain, uses, i, j):
            in_group = (len(uses) + 1 - i % 2) // 2
            eng.wait_ge(s[f"{chain}{i % 2}_full"], j * in_group + i // 2 + 1)

        A_XNT, A_SSQ, A_X, A_Z, A_PROJ, A_DTT, A_BCT, A_DT = 0, 1, 2, 4, 6, 7, 8, 9
        C_OUT, C_SSQ, C_FFN, C_DOWN, C_OGT, C_N2T, C_BACK, C_LOGIT, C_RANK, C_SHARED_FFN, C_SHARED = (
            0, 1, 2, 10, 11, 12, 13, 14, 15, 16, 24)

        def chained(eng, name, per_group):
            done = [0]

            def link(j, ins):
                i = done[0] % per_group
                done[0] += 1
                ins.then_inc(s[name], 1)
                eng.wait_ge(s[name], j * per_group + i + 1)
            return link

        def now(eng, value):
            return value if isinstance(value, int) else eng.to_reg(value)

        def apart(eng):
            eng.wait_ge(s["pool_setup"], POOL_SETUP)

        def hc_of(g, n):
            dve_n = [m for m in range(NS) if m not in POOL_N]
            if n in POOL_N:
                return s["hc_pool"], g * len(POOL_N) + POOL_N.index(n) + 1
            return s["hc_dve"], g * len(dve_n) + dve_n.index(n) + 1

        def back(g, n, k):
            g, n = (g, n - k) if n >= k else (g - 1, n - k + NS)
            return None if isinstance(g, int) and g < 0 else (g, n)

        def wait_hc(eng, step):
            if step is not None:
                eng.wait_ge(*hc_of(*step))

        def groups(eng, body):
            body(0, 0, True, False)
            with eng.Fori(0, (G - 2) // 2) as i:
                body(2 * i + 1, 1, True, True)
                body(2 * i + 2, 0, True, True)
            body(G - 1, (G - 1) % 2, False, True)

        LAST = (TILES // U - 1, U - 1)

        def after(i, r):
            return (i, r + 1) if r + 1 < U else (i + 1, 0)

        def turns(eng, step):
            with eng.Fori(0, TILES // U - 1) as i:
                for r in range(U):
                    step(after(i, r), (i, r), after(*after(i, r)))
            last = TILES // U - 1
            for r in range(U - 1):
                step((last, r + 1), (last, r), (last, r + 2) if r + 2 < U else None)

        def wait_c(eng, g, n):
            eng.wait_ge(s[f"c_in{n % RING_C}"], 16 * (g * (NS // RING_C) + n // RING_C + 1))

        block = ctx.enter_context(nc.Block())

        @block.sync
        def _(sp):
            def load(dst, src, sem):
                sp.dma_start(dst, src).then_inc(s[sem], 16)

            x_v = io["L0_attn_hidden_states"].rearrange("b (t p) d -> p (b t) d", p=P)
            load(x_all[:, 0:TG, :], x_v[:, 0:TG, :], "x_first_in")
            load(c_sb[:, :], io["L0_c"], "cond_in")
            load(wmod, io["L0_wmod"], "cond_in")
            small = [
                (w_in[:, :], io["L0_attn_in_proj_w"]),
                (ln_in[:, :], io["L0_attn_input_ln_w"].rearrange("(p o) -> p o", o=1)),
                (conv_w[:, :, :], io["L0_attn_conv_w"].rearrange("(h p) k -> p h k", p=P)),
                (conv_b[:, :], io["L0_attn_conv_b"]),
                (w_xp[:, :, :], io["L0_attn_x_proj_w"].rearrange("(h p) c -> p h c", p=P)),
                (ln_dt[:, :], io["L0_attn_dt_ln_w"].rearrange("(p o) -> p o", o=1)),
                (ln_bc[:, 0:NS], io["L0_attn_b_ln_w"].partition_broadcast(P)),
                (ln_bc[:, NS:BC], io["L0_attn_c_ln_w"].partition_broadcast(P)),
                (w_dt[:, :], io["L0_attn_dt_proj_w"]),
                (dt_b[:, :], io["L0_attn_dt_proj_b"]),
                (neg_a[:, :, :], io["L0_attn_A_log"].rearrange("(h p) n -> p h n", p=P)),
                (d_skip[:, :], io["L0_attn_D_skip"]),
                (w_out[:, :, :], io["L0_attn_out_proj_w"].rearrange("(h p) d -> p h d", p=P)),
                (ln_moe[:, :], io["L0_attn_pre_moe_ln_w"].rearrange("(p o) -> p o", o=1)),
                (w_gate[:, :], io["L0_attn_gate_w"]),
                (w_up[:, :], io["L0_attn_up_w"]),
                (w_down[:, :, :], io["L0_attn_down_w"].rearrange("(c p) d -> p c d", p=P)),
                (w1s[:, :], io["L0_ffn_w1s"]),
                (w2s[:, :], io["L0_ffn_w2s"]),
                (w3s[:, :, :], io["L0_ffn_w3s"].rearrange("(c p) d -> p c d", p=P)),
                (w_route[:, :], io["L0_ffn_Wg"]),
            ]
            assert 16 * len(small) == WEIGHTS
            for dst, src in small:
                load(dst, src, "weights_in")
            for j in range(1, G):
                load(x_all[:, j * TG:(j + 1) * TG, :], x_v[:, j * TG:(j + 1) * TG, :], "x_rest_in")
            for e in range(NE):
                load(e_w1[:, e, :], io["L0_ffn_W1"][e, :, :], "experts_in")
            sp.wait_ge(s["pool_setup"], POOL_SETUP)
            load(xs_rows[SPARE:SPARE + NE * P, :].rearrange("(e p) d -> p e d", p=P), blank, "zeros_out")

            def c_out(j, q):
                sp.wait_ge(s["a_dtnt"], j + 1)
                sp.dma_start(c_rows[q], dtn_t[R:R + NS, :]).then_inc(s["c_rows_out"], 16)

            def body(g, q, has_a, has_c):
                written = now(sp, 16 * (g + 1))
                for n in range(NS):
                    read = None
                    if back(g, n, RING_C) is not None:
                        sem, value = hc_of(*back(g, n, RING_C))
                        read = (sem, now(sp, value))
                    if n == 0:
                        sp.wait_ge(s["c_rows_out"], written)
                    if read is not None:
                        sp.wait_ge(*read)
                    sp.dma_start(cs[:, n % RING_C, :], c_rows[q, n].partition_broadcast(P)).then_inc(s[f"c_in{n % RING_C}"], 16)
                    if has_a and n == NS - 2:
                        c_out(g + 1, 1 - q)

            c_out(0, 0)
            groups(sp, body)

            sp.wait_ge(s["u_ready"], G)
            sp.wait_ge(s["bc_parts"], G)
            for e in range(NE):
                load(e_w2[:, e, :], io["L0_ffn_W2"][e, :, :], "late_experts_in")
                load(e_w3[:, e, :, :], io["L0_ffn_W3"][e, :, :].rearrange("(c p) d -> p c d", p=P), "late_experts_in")

            sp.wait_ge(s["tables"], 1)
            sp.wait_ge(s["scattered"], 16 * NT)
            sp.wait_ge(s["tails_out"], 16 * NE)
            sp.wait_ge(s["zeros_out"], 16)

            def load_tile(i, r):
                row = sp.value_load(row_tab[0:1, bass.ds(U * i + r, 1)], min_val=0, max_val=SPARE + (NE - 1) * P)
                before = U * i + r - U + 1
                positive(sp, s["xt_read"], before)
                positive(sp, s["numbered"], before)
                sp.dma_start(xt[:, r, :], xs_rows[bass.ds(row, P), :]).then_inc(s[f"xt_in{r}"], 16)

            for r in range(U):
                load_tile(0, r)
            with sp.Fori(1, TILES // U) as i:
                for r in range(U):
                    load_tile(i, r)

            for r in range(2):
                sp.wait_ge(s[f"ys_out{r}"], 16 * (TILES // 2))
            y_v = ys_rows[0:NT * P, :].rearrange("(t p) d -> p t d", p=P)
            for j in range(G):
                load(y_rows[:, j * TG:(j + 1) * TG, :], y_v[:, j * TG:(j + 1) * TG, :], f"gathered{j}")

            out_v = out.rearrange("b (t p) d -> p (b t) d", p=P)
            for j in range(G):
                sp.wait_ge(s["final_sum"], j + 1)
                sp.dma_start(out_v[:, j * TG:(j + 1) * TG, :], x_all[:, j * TG:(j + 1) * TG, :]).then_inc(s["out_done"], 16)
            sp.wait_ge(s["out_done"], 16 * G)


        @block.gpsimd
        def _(pool):
            count = [0]

            def setup(ins):
                count[0] += 1
                ins.then_inc(s["pool_setup"], 1)
                pool.wait_ge(s["pool_setup"], count[0])

            def diagonal(t, base, cols):
                setup(pool.affine_select(out=t, in_=t, compare_op=ALU.not_equal, fill=1.0, base=-base,
                                         pattern=[[-1, cols]], channel_multiplier=1))

            setup(pool.memset(ident[:, :], 0.0))
            diagonal(ident[:, :], 0, P)
            setup(pool.memset(eps_ln[:, :], EPS_LN))
            setup(pool.memset(eps_rms[:, :], EPS_RMS))
            setup(pool.memset(one[:, :], 1.0))
            setup(pool.memset(ones[:, :], 1.0))
            setup(pool.memset(identb[:, :], 0.0))
            diagonal(identb[:, :], 0, P)
            setup(pool.memset(sel[:, :], 0.0))
            for k in range(3):
                diagonal(sel[:, :], NS * k, NS)
            setup(pool.memset(onesb[:, :], 1.0))
            setup(pool.memset(tri[:, :], 1.0))
            setup(pool.affine_select(out=tri[:, :], in_=tri[:, :], compare_op=ALU.is_gt, fill=0.0, base=0,
                                     pattern=[[1, P]], channel_multiplier=-1))
            setup(pool.memset(blank, 0.0))
            setup(pool.memset(ones8[:, :], 1.0))
            setup(pool.memset(base5[:, :, :], 0.0))
            setup(pool.iota(iota_i[:, :], [[1, NUMBERS]], base=0, channel_multiplier=0))
            setup(pool.tensor_copy(iota_j[:, :], iota_i[:, :]))
            setup(pool.iota(iota_i[:, 0:1], [[1, 1]], base=0, channel_multiplier=1))
            setup(pool.tensor_copy(pid[:, :], iota_i[:, 0:1]))
            setup(pool.tensor_scalar(iota_k[:, :], iota_j[:, :], float(P), None, ALU.mult))
            setup(pool.tensor_scalar(token[:, :], iota_k[:, :], pid[:, :], None, ALU.add))
            setup(pool.tensor_copy(blank[:, :, D], token[:, NT + NE:NUMBERS]))
            setup(pool.tensor_scalar(region[:, :], iota_j[:, 0:NE], float(REG), None, ALU.mult))
            setup(pool.tensor_scalar(rev[:, :], iota_j[:, 0:NE], -1.0, float(NE), ALU.mult, ALU.add))
            assert count[0] == POOL_SETUP

            def scan(g, q, n):
                if n not in POOL_N:
                    return
                wait_c(pool, g, n)
                pool.wait_ge(s["h_done"], g * NS + n + 1)
                positive(pool, s["nsum_done"], g * NS + n - RING_P + 1)
                pool.tensor_tensor(hc[:, n % RING_P], hs[:, n % RING_H],
                                   cs[:, n % RING_C].unsqueeze(1).broadcast_to([P, H, GT]), ALU.mult)\
                    .then_inc(s["hc_pool"], 1)

            def c_scatter(j):
                apart(pool)
                pool.wait_ge(s["c_slot"], j + 1)
                pool.wait_ge(s["c_h2tok"], j + 1)
                for t in range(TG):
                    pool.indirect_dma_start(out=xs_rows, out_offset=bass.IndirectOffsetOnAxis(ap=slot[:, t:t + 1], axis=0),
                                            in_=h2_tok[:, t, :], in_offset=None).then_inc(s["scattered"], 16)

            def body(g, q, has_a, has_c):
                for n in range(NS):
                    scan(g, q, n)
                    if has_c and n == 13:
                        c_scatter(g - 1)

            pool.wait_ge(s["zeros_out"], 16)
            groups(pool, body)
            c_scatter(G - 1)

            pool.wait_ge(s["nsum_done"], G * NS)
            pool.memset(blank, 0.0).then_inc(s["pool_setup"], 1)
            pool.wait_ge(s["pool_setup"], POOL_SETUP + 1)
            pool.tensor_copy(blank[:, :, D], token[:, NT:NT + NE]).then_inc(s["pool_setup"], 1)
            pool.wait_ge(s["pool_setup"], POOL_SETUP + 2)
            pool.wait_ge(s["tail_idx"], 1)
            for e in range(NE):
                pool.indirect_dma_start(out=xs_rows, out_offset=bass.IndirectOffsetOnAxis(ap=tail[:, e:e + 1], axis=0),
                                        in_=blank[:, e, :], in_offset=None).then_inc(s["tails_out"], 16)

            def store(i, r):
                stored, made = now(pool, 16 * (U // 2 * i + r // 2)), now(pool, U * i + r + 1)
                b = r % 2
                apart(pool)
                positive(pool, s[f"ys_out{b}"], stored)
                pool.wait_ge(s["numbered"], made)
                pool.tensor_copy(row_idx[:, b:b + 1], number[:, bass.ds(U * i + r, 1)]).then_inc(s["row_idx"], 1)
                apart(pool)
                pool.wait_ge(s["row_idx"], made)
                pool.wait_ge(s["yo"], made)
                pool.indirect_dma_start(out=ys_rows, out_offset=bass.IndirectOffsetOnAxis(ap=row_idx[:, b:b + 1], axis=0),
                                        in_=yo[:, b, :], in_offset=None).then_inc(s[f"ys_out{b}"], 16)

            for r in range(U):
                store(0, r)
            with pool.Fori(1, TILES // U) as i:
                for r in range(U):
                    store(i, r)

        @block.tensor
        def _(pe):
            mm = pe.matmul

            pe.wait_ge(s["pool_setup"], POOL_SETUP)
            pe.wait_ge(s["silu_c"], 1)
            pe.transpose(Y[0][:, 0:B], c_silu[:, :], ident[0:B, 0:B]).then_inc(s["silu_ct_ps"], 1)
            pe.wait_ge(s["silu_ct"], 1)
            pe.wait_ge(s["cond_in"], 32)
            for m in range(6):
                mm(Y[0][:, m * B:(m + 1) * B], wmod[:, m * D:(m + 1) * D], c_t[:, :], start=True, stop=True)
            mm(Y[0][0:B, P:P + D], c_t[:, :], wmod[:, 5 * D:6 * D], start=True, stop=True).then_inc(s["mod_ps"], 1)
            pe.wait_ge(s["dve_setup"], GATE_ROWS)
            for r in range(B // 4):
                positive(pe, s["gate_read"], r - 1)
                for b in range(4):
                    last = mm(Y[(r + 1) % 2][:, b * D:(b + 1) * D], ident[0:B, 4 * r + b:4 * r + b + 1].broadcast_to([B, P]),
                              gate16[:, :], start=True, stop=True)
                last.then_inc(s["gate_ps"], 1)
            pe.wait_ge(s["weights_in"], WEIGHTS)
            pe.wait_ge(s["dve_setup"], DVE_SETUP)
            pe.wait_ge(s["gate_read"], B // 4)

            def a_take(i, j):
                take(pe, A_FREED, i, j)
                return AW[i % 2]

            def c_take(i, j):
                take(pe, C_FREED, i, j)
                return CW[i % 2]

            def a_xnt(j):
                pe.wait_ge(s["a_xn"], j + 1)
                w = a_take(A_XNT, j)
                for t in range(TG):
                    last = pe.transpose(w[:, t * P:(t + 1) * P], xn[:, t, :], ident[:, :])
                last.then_inc(s["a0_full"], 1)

            def a_ssq(j):
                pe.wait_ge(s["a_sq"], j + 1)
                mm(a_take(A_SSQ, j)[:, :], ones[:, :], sq_a, start=True, stop=True).then_inc(s["a1_full"], 1)

            def a_in(j, first):
                pe.wait_ge(s["a_hn"], j + 1)
                for h in range(2):
                    c = h if first == A_X else 2 + h
                    mm(a_take(first + h, j)[:, :], w_in[:, c * P:(c + 1) * P], hn, start=True, stop=True)\
                        .then_inc(s[f"a{h}_full"], 1)

            def a_proj(j, q):
                pe.wait_ge(s["a_silu"], j + 1)
                w = a_take(A_PROJ, j)
                for t in range(TG):
                    for h in range(H):
                        last = mm(w[:, t * XP:(t + 1) * XP], xs_[:, q, h, t * P:(t + 1) * P], w_xp[:, h, :],
                                  start=(h == 0), stop=(h == H - 1))
                last.then_inc(s["a0_full"], 1)

            def a_dtbc_t(j):
                apart(pe)
                pe.wait_ge(s["a_dtn"], j + 1)
                w = a_take(A_DTT, j)
                for t in range(TG):
                    last = pe.transpose(w[0:R + NS, t * P:(t + 1) * P], dtc[:, t, :], ident[:, :])
                last.then_inc(s["a1_full"], 1)
                apart(pe)
                pe.wait_ge(s["a_parts"], j + 1)
                wb = a_take(A_BCT, j)[:, :].bitcast(BF16)
                for t in range(TG):
                    last = pe.transpose(wb[0:3 * NS, t * P:(t + 1) * P], parts_tok[:, t, :], identb[:, :])
                last.then_inc(s["a0_full"], 1)

            def a_dt(j):
                pe.wait_ge(s["a_dtnt"], j + 1)
                for h in range(H):
                    mm(a_take(A_DT + h, j)[:, :], w_dt[:, h * P:(h + 1) * P], dtn_t[0:R, :], start=True, stop=True)\
                        .then_inc(s[f"a{(A_DT + h) % 2}_full"], 1)

            def c_out(j, q):
                pe.wait_ge(s["yg_ready"], j + 1)
                w = c_take(C_OUT, j)
                for h in range(H):
                    mm(w[:, :], w_out[:, h, :], yt[:, h, :], start=(h == 0), stop=False)
                mm(w[:, :], ident[:, :], h_t[:, q, :], start=False, stop=True).then_inc(s["c0_full"], 1)

            def c_ssq(j):
                pe.wait_ge(s["c_sq"], j + 1)
                mm(c_take(C_SSQ, j)[:, :], ones[:, :], tmp_c[:, :], start=True, stop=True).then_inc(s["c1_full"], 1)

            def c_chunk(j, first, side, w, k, rhs):
                use = first + 2 * k + side
                mm(c_take(use, j)[:, :], w[:, k * P:(k + 1) * P], rhs, start=True, stop=True)\
                    .then_inc(s[f"c{use % 2}_full"], 1)

            def c_dense(j, side, k):
                if k == 0:
                    pe.wait_ge(s["c_hn"], j + 1)
                c_chunk(j, C_FFN, side, (w_gate, w_up)[side], k, tmp_c[:, :])

            def c_expert(j, side, k):
                c_chunk(j, C_SHARED_FFN, side, (w1s, w2s)[side], k, h2_t[:, :])

            def c_down(j):
                pe.wait_ge(s["c_prod"], j * FC + FC)
                w = c_take(C_DOWN, j)
                for f in range(FC):
                    mm(w[:, :], w_down[:, f, :], prod_c[:, f, :], start=(f == 0), stop=False)
                mm(w[:, :], ident[:, :], hid[:, :], start=False, stop=True).then_inc(s["c0_full"], 1)

            def c_ogt(j):
                pe.wait_ge(s["c_scaled"], j + 1)
                w = c_take(C_OGT, j)
                for t in range(TG):
                    last = pe.transpose(w[:, t * P:(t + 1) * P], act_c[:, 0, t * P:(t + 1) * P], ident[:, :])
                last.then_inc(s["c1_full"], 1)

            def c_n2t(j):
                pe.wait_ge(s["c_n2"], j + 1)
                w = c_take(C_N2T, j)
                for t in range(TG):
                    last = pe.transpose(w[:, t * P:(t + 1) * P], n2[:, t, :], ident[:, :])
                last.then_inc(s["c0_full"], 1)

            def c_back(j):
                pe.wait_ge(s["c_h2t"], j + 1)
                w = c_take(C_BACK, j)
                for t in range(TG):
                    last = pe.transpose(w[:, t * P:(t + 1) * P], h2_t[:, t * P:(t + 1) * P], ident[:, :])
                last.then_inc(s["c1_full"], 1)

            def c_logit(j):
                w = c_take(C_LOGIT, j)
                for t in range(TG):
                    last = mm(w[:, t * NE:(t + 1) * NE], h2_t[:, t * P:(t + 1) * P], w_route[:, :], start=True, stop=True)
                last.then_inc(s["c0_full"], 1)

            def c_rank(j):
                pe.wait_ge(s["c_onehot"], j + 1)
                w = c_take(C_RANK, j)
                oh = onehot[:, :, :].rearrange("p t e -> p (t e)")
                mm(w[:, 0:TG * NE], tri[:, :], oh, start=True, stop=True)
                mm(w[:, TG * NE:2 * TG * NE], onesb[:, :], oh, start=True, stop=True).then_inc(s["c1_full"], 1)

            def c_shared(j):
                pe.wait_ge(s["c_sprod"], j * FC + FC)
                w = c_take(C_SHARED, j)
                for t in range(TG):
                    for f in range(FC):
                        last = mm(w[:, t * D:(t + 1) * D], prod_c[:, f, t * P:(t + 1) * P], w3s[:, f, :],
                                  start=(f == 0), stop=(f == FC - 1))
                last.then_inc(s["c0_full"], 1)

            def start_y(g, q):
                positive(pe, s["yg_ready"], g)
                for h in range(H):
                    mm(Y[h][:, :], d_diag[:, h, :], xs_[:, q, h, :], start=True, stop=False)

            def sum_state(g, n):
                wait_hc(pe, (g, n))
                for h in range(H):
                    last = mm(Y[h][:, :], ident[:, :], hc[:, n % RING_P, h, :], start=False, stop=(n == NS - 1))
                last.then_inc(s["nsum_done"], 1)

            def b_row(g, q, n):
                if n == 0:
                    pe.wait_ge(s["bc_parts"], g + 1)
                if back(g, n, 2) is not None:
                    pe.wait_ge(s["bx_done"], g * NS + n - 1)
                mm(BB[n % 2][:, :], sel[:, n:n + 1].broadcast_to([3 * NS, P]), parts_t[:, q, :], start=True, stop=True)\
                    .then_inc(s["b_full"], 1)

            def steps(n, g, q, has_scan, has_a, has_c):
                ja, qa, jc = g + 1, 1 - q, g - 1

                def a(part, *args):
                    if has_a:
                        part(ja, *args)

                def c(part, *args):
                    if has_c:
                        part(jc, *args)

                def b():
                    if has_scan and n + 2 < NS:
                        b_row(g, q, n + 2)
                    elif has_scan and has_a:
                        b_row(ja, qa, n + 2 - NS)

                def total(k):
                    if has_scan and back(g, n, k) is not None:
                        sum_state(*back(g, n, k))

                b()
                if n == 0:
                    total(2), total(1)
                elif n == 2:
                    c(c_out, qa)
                    if has_scan:
                        start_y(g, q)
                    total(2), a(a_xnt)
                elif n == 3:
                    total(2), c(c_ssq), a(a_ssq)
                elif n == 4:
                    total(2)
                elif n == 5:
                    a(a_in, A_X), c(c_dense, 0, 0), c(c_dense, 1, 0), a(a_in, A_Z), total(2)
                elif n == 6:
                    c(c_dense, 0, 1), c(c_dense, 1, 1), total(2), c(c_dense, 0, 2)
                elif n == 7:
                    c(c_dense, 1, 2), c(c_dense, 0, 3), total(2), c(c_dense, 1, 3)
                elif n == 8:
                    a(a_proj, qa), c(c_down), total(2)
                elif n == 9:
                    total(2), c(c_ogt)
                elif n == 10:
                    a(a_dtbc_t), total(2)
                elif n == 11:
                    a(a_dt), total(2), c(c_n2t), c(c_logit), c(c_back)
                elif n == 12:
                    c(c_rank), c(c_expert, 0, 0), total(2)
                elif n == 13:
                    c(c_expert, 1, 0), c(c_expert, 0, 1), c(c_expert, 1, 1), total(2), c(c_expert, 0, 2)
                elif n == 14:
                    c(c_expert, 1, 2), c(c_expert, 0, 3), total(2), c(c_expert, 1, 3)
                elif n == 15:
                    c(c_shared), total(2)

            def body(g, q, has_a, has_c):
                for n in range(NS):
                    steps(n, g, q, True, has_a, has_c)

            for n in range(NS):
                steps(n, -1, 1, False, True, False)
            b_row(0, 0, 0)
            b_row(0, 0, 1)
            groups(pe, body)
            sum_state(G - 1, NS - 2)
            sum_state(G - 1, NS - 1)
            for n in range(NS):
                steps(n, G, 0, False, False, True)

            XT_B, PT_B, DOWN_B = bank[0], bank[1], bank[2]
            UP1, UP2 = bank[3:5], bank[5:7]

            def e_transpose(i, r):
                pe.wait_ge(s[f"xt_in{r}"], 16 * i + 16)
                positive(pe, s["ext"], U * i + r)
                pe.transpose(XT_B[:, 0:P], xt[:, r, 0:D], ident[:, :]).then_inc(s["xt_read"], 1)

            def e_up(i, r, w, banks, done, freed, e):
                positive(pe, s[freed], U * i + r - 1)
                mm(banks[r % 2][:, :], ext[:, r % 2, :], w[:, bass.ds(e, 1), :].rearrange("p o f -> p (o f)"),
                   start=True, stop=True).then_inc(s[done], 1)

            def e_prod_t(i, r):
                pe.wait_ge(s["prod_done"], U * i + r + 1)
                positive(pe, s["prodt"], U * i + r)
                for f in range(FC):
                    last = pe.transpose(PT_B[:, f * P:(f + 1) * P], pe_[:, r % 2, f * P:(f + 1) * P], ident[:, :])
                last.then_inc(s["prodt_ps"], 1)

            def e_down(i, r, e):
                pe.wait_ge(s["prodt"], U * i + r + 1)
                positive(pe, s["yo"], U * i + r)
                for f in range(FC):
                    last = mm(DOWN_B[:, 0:D], pet[:, r % 2, f * P:(f + 1) * P],
                              e_w3[:, bass.ds(e, 1), f, :].rearrange("p o d -> p (o d)"), start=(f == 0), stop=(f == FC - 1))
                last.then_inc(s["down_ps"], 1)

            def expert_of(i, r):
                return pe.value_load(exp_tab[0:1, bass.ds(U * i + r, 1)], min_val=0, max_val=NE - 1)

            held = {}

            def e_step(tile, before, behind):
                first = before is None or before[1] == 0
                e_before = None if before is None else expert_of(*before) if first else held["before"]
                e = expert_of(*tile) if first else held["tile"]
                if behind is not None:
                    e_transpose(*behind)
                pe.wait_ge(s["ext"], U * tile[0] + tile[1] + 1)
                e_up(*tile, e_w1, UP1, "up1_ps", "gelu_done", e)
                if before is not None and before[1] + 2 <= U and behind is not None:
                    held["tile"] = expert_of(*behind)
                held["before"] = e
                if before is not None:
                    e_prod_t(*before)
                e_up(*tile, e_w2, UP2, "up2_ps", "prod_done", e)
                if before is not None:
                    e_down(*before, e_before)

            pe.wait_ge(s["tables"], 1)
            pe.wait_ge(s["experts_in"], 16 * NE)
            pe.wait_ge(s["late_experts_in"], 32 * NE)
            pe.wait_ge(s["base_ready"], G)
            e_transpose(0, 0)
            e_step((0, 0), None, (0, 1))
            turns(pe, e_step)
            e_prod_t(*LAST)
            e_down(*LAST, expert_of(*LAST))

        @block.scalar
        def _(act):
            f = act.activation

            act.wait_ge(s["cond_in"], 32)
            f(c_silu[:, :], c_sb[:, :], ACT.Silu).then_inc(s["silu_c"], 1)
            act.wait_ge(s["silu_ct_ps"], 1)
            f(c_t[:, :], Y[0][:, 0:B], ACT.Copy).then_inc(s["silu_ct"], 1)
            act.wait_ge(s["weights_in"], WEIGHTS)
            act.preload_act_table_set(EXP_LN)
            f(neg_a[:, :, :], neg_a[:, :, :], ACT.Exp).then_inc(s["exp_a"], 1)
            act.wait_ge(s["pool_setup"], POOL_SETUP)
            act.wait_ge(s["dve_setup"], DVE_SETUP)

            link_a = chained(act, "a_act", 3)
            link_c = chained(act, "c_act", 1)

            def a_rstd(j):
                act.wait_ge(s["a_mv"], j + 1)
                link_a(j, f(rstd_a[:, :], mv_a[:, 1, :], ACT.Ln, scale=1.0 / D, bias=eps_ln[:, :]))
                f(rstd_a[:, :], rstd_a[:, :], ACT.Exp, scale=-0.5).then_inc(s["a_rstd"], 1)

            def normalised(j, dst, mv, rstd, chain, done):
                made = now(act, j + 1)
                apart(act)
                act.wait_ge(s[chain + "_shift"], made)
                for t in range(TG):
                    last = f(dst[:, t, :], x_all[:, bass.ds(j * TG + t, 1), :].rearrange("p o d -> p (o d)"), ACT.Identity,
                             scale=rstd[:, t:t + 1], bias=mv[:, 2, t:t + 1])
                last.then_inc(s[done], 1)

            def a_h(j, q):
                filled(act, "a", A_FREED, A_XNT, j)
                positive(act, s["hid_ready"], j - 1)
                for b in range(GB):
                    last = f(h_t[:, q, b * S:(b + 1) * S], AW[0][:, b * S:(b + 1) * S], ACT.Identity,
                             scale=a_mod[:, 1, b:b + 1], bias=a_mod[:, 0, b:b + 1])
                last.then_inc(s["a_h"], 1)
                act.wait_ge(s["a_h"], j + 1)
                f(sq_a, h_t[:, q, :], ACT.Square).then_inc(s["a_sq"], 1)

            def a_rms(j):
                filled(act, "a", A_FREED, A_SSQ, j)
                positive(act, s["a_hn"], j)
                f(rms_a, AW[1][:, :], ACT.Ln, scale=1.0 / D, bias=eps_rms[:, :]).then_inc(s["a_ln"], 1)
                act.wait_ge(s["a_ln"], j + 1)
                f(rms_a, rms_a, ACT.Exp, scale=-0.5).then_inc(s["a_rms"], 1)

            def a_xcopy(j):
                positive(act, s["a_conv"], j)
                positive(act, s["a_silu"], j)
                for h in range(H):
                    filled(act, "a", A_FREED, A_X + h, j)
                    f(conv[:, h], AW[h][:, :].rearrange("p (b t) -> p b t", b=GB), ACT.Identity,
                      scale=conv_w[:, h, K - 1:K], bias=conv_b[:, h:h + 1])
                    f(xpad[:, h, :, K - 1:PAD], AW[h][:, :].rearrange("p (b t) -> p b t", b=GB), ACT.Copy)\
                        .then_inc(s["a_xpad"], 1)

            def a_silu_z(j, q):
                positive(act, s["yg_ready"], j - 1)
                for h in range(H):
                    filled(act, "a", A_FREED, A_Z + h, j)
                    f(zs[:, q, h, :], AW[h][:, :], ACT.Silu).then_inc(s["a_zs"], 1)

            def a_silu_x(j, q):
                act.wait_ge(s["a_conv"], j + 1)
                f(xs_[:, q, :, :].rearrange("p h t -> p (h t)"), conv.rearrange("p h b t -> p (h b t)"), ACT.Silu)\
                    .then_inc(s["a_silu"], 1)

            def a_proj_copy(j):
                filled(act, "a", A_FREED, A_PROJ, j)
                w = AW[0][:, 0:TG * XP].rearrange("p (t c) -> p t c", t=TG)
                f(proj_sq, w, ACT.Square)
                f(proj, w, ACT.Copy).then_inc(s["a_proj_copy"], 1)

            def a_proj_rs(j):
                act.wait_ge(s["a_proj_ms"], j + 1)
                f(proj_rs[:, 0, :], proj_ms[:, 0, :], ACT.Ln, scale=1.0 / R, bias=eps_rms[:, :])
                link_a(j, f(proj_rs[:, 1:3, :], proj_ms[:, 1:3, :], ACT.Ln, scale=1.0 / NS, bias=eps_rms[:, :]))
                f(proj_rs[:, :, :], proj_rs[:, :, :], ACT.Exp, scale=-0.5).then_inc(s["a_proj_rs"], 1)

            def a_transposed(j, q):
                filled(act, "a", A_FREED, A_DTT, j)
                positive(act, s["c_rows_out"], 16 * j)
                f(dtn_t[0:R + NS, :], AW[1][0:R + NS, :], ACT.Copy, scale=1.0).then_inc(s["a_dtnt"], 1)
                filled(act, "a", A_FREED, A_BCT, j)
                f(parts_t[:, q, :], AW[0][:, :].bitcast(BF16)[0:3 * NS, 0:GT], ACT.Copy).then_inc(s["bc_parts"], 1)

            def a_soft(j):
                positive(act, s["dt_ready"], j)
                for h in range(H):
                    filled(act, "a", A_FREED, A_DT + h, j)
                    w = AW[(A_DT + h) % 2]
                    last = f(soft[:, h, :], w[:, :], ACT.Abs, bias=dt_b[:, h:h + 1])
                    f(relu[:, h, :], w[:, :], ACT.Relu, bias=dt_b[:, h:h + 1]).then_inc(s["a_relu"], 1)
                act.wait_ge(s["a_relu"], H * (j + 1))
                link_a(j, f(soft, soft, ACT.Exp, scale=-1.0))
                f(soft, soft, ACT.Ln, bias=one[:, :]).then_inc(s["a_soft"], 1)

            def c_hid(j):
                filled(act, "c", C_FREED, C_OUT, j)
                f(hid[:, :], CW[0][:, :], ACT.Copy).then_inc(s["hid_ready"], 1)
                f(tmp_c[:, :], CW[0][:, :], ACT.Square).then_inc(s["c_sq"], 1)

            def c_rms(j):
                filled(act, "c", C_FREED, C_SSQ, j)
                f(rms_c[:, :], CW[1][:, :], ACT.Ln, scale=1.0 / D, bias=eps_rms[:, :]).then_inc(s["c_ln"], 1)
                act.wait_ge(s["c_ln"], j + 1)
                f(rms_c[:, :], rms_c[:, :], ACT.Exp, scale=-0.5).then_inc(s["c_rms"], 1)

            def c_act(j, first, k, func, done, read):
                filled(act, "c", C_FREED, first + 2 * k, j)
                if k >= 2:
                    act.wait_ge(s[read], j * FC + k - 1)
                f(act_c[:, k % 2, :], CW[0][:, :], func).then_inc(s[done], 1)

            def c_silu_(j, k):
                c_act(j, C_FFN, k, ACT.Silu, "c_silu", "c_prod")

            def c_gelu_(j, k):
                c_act(j, C_SHARED_FFN, k, ACT.Gelu, "c_gelu", "c_sprod")

            def c_scale(j):
                filled(act, "c", C_FREED, C_DOWN, j)
                for b in range(GB):
                    last = f(act_c[:, 0, b * S:(b + 1) * S], CW[0][:, b * S:(b + 1) * S], ACT.Copy, scale=c_mod[:, 2, b:b + 1])
                last.then_inc(s["c_scaled"], 1)

            def c_rstd(j):
                act.wait_ge(s["c_mv"], j + 1)
                link_c(j, f(rstd_c[:, :], mv_c[:, 1, :], ACT.Ln, scale=1.0 / D, bias=eps_ln[:, :]))
                f(rstd_c[:, :], rstd_c[:, :], ACT.Exp, scale=-0.5).then_inc(s["c_rstd"], 1)

            def c_h2t(j):
                filled(act, "c", C_FREED, C_N2T, j)
                for b in range(GB):
                    last = f(h2_t[:, b * S:(b + 1) * S], CW[0][:, b * S:(b + 1) * S], ACT.Identity,
                             scale=c_mod[:, 4, b:b + 1], bias=c_mod[:, 3, b:b + 1])
                last.then_inc(s["c_h2t"], 1)

            def c_h2tok(j):
                filled(act, "c", C_FREED, C_BACK, j)
                positive(act, s["scattered"], 16 * TG * j)
                f(h2_tok[:, :, 0:D], CW[1][:, :].rearrange("p (t d) -> p t d", t=TG), ACT.Copy).then_inc(s["c_h2tok"], 1)

            def decay(g, q, n):
                if n == 0:
                    act.wait_ge(s["dt_ready"], g + 1)
                positive(act, s["h_done"], g * NS + n - RING_A + 1)
                for h in range(H):
                    last = f(da[:, n % RING_A, h, :, 1:S], dt[:, q, h, :].rearrange("p (b t) -> p b t", b=GB)[:, :, 1:S],
                             ACT.Exp, scale=neg_a[:, h, n:n + 1])
                last.then_inc(s["da_ready"], 1)

            def steps(n, g, q, has_scan, has_a, has_c):
                ja, qa, jc = g + 1, 1 - q, g - 1

                def a(part, *args):
                    if has_a:
                        part(ja, *args)

                def c(part, *args):
                    if has_c:
                        part(jc, *args)

                def da(k):
                    if has_scan and k < NS:
                        decay(g, q, k)
                    elif has_scan and has_a:
                        decay(ja, qa, k - NS)

                if n == 0:
                    da(2)
                elif n == 1:
                    a(a_rstd), da(3)
                elif n == 2:
                    a(normalised, xn, mv_a, rstd_a, "a", "a_xn"), da(4), c(c_hid)
                elif n == 3:
                    a(a_h, qa), da(5), c(c_rms)
                elif n == 4:
                    a(a_rms), da(6), da(7)
                elif n == 5:
                    da(8), a(a_xcopy), c(c_silu_, 0)
                elif n == 6:
                    c(c_silu_, 1), a(a_silu_z, qa), c(c_silu_, 2)
                elif n == 7:
                    a(a_silu_x, qa), c(c_silu_, 3)
                    act.preload_act_table_set(EXP_LN)
                elif n == 8:
                    da(9), a(a_proj_copy), da(10)
                elif n == 9:
                    a(a_proj_rs), c(c_scale), da(11)
                elif n == 10:
                    c(c_rstd), a(a_transposed, qa), da(12), da(13)
                elif n == 11:
                    c(normalised, n2, mv_c, rstd_c, "c", "c_n2"), c(c_h2t), c(c_h2tok), da(14), a(a_soft)
                elif n == 12:
                    da(15), c(c_gelu_, 0)
                elif n == 13:
                    c(c_gelu_, 1), c(c_gelu_, 2)
                elif n == 14:
                    c(c_gelu_, 3)
                    act.preload_act_table_set(EXP_LN)
                elif n == 15:
                    da(16), da(17)

            def body(g, q, has_a, has_c):
                for n in range(NS):
                    steps(n, g, q, True, has_a, has_c)

            for n in range(NS):
                steps(n, -1, 1, False, True, False)
            decay(0, 0, 0)
            decay(0, 0, 1)
            groups(act, body)
            for n in range(NS):
                steps(n, G, 0, False, False, True)

            def e_ext(i, r):
                act.wait_ge(s["xt_read"], U * i + r + 1)
                positive(act, s["up2_ps"], U * i + r - 1)
                f(ext[:, r % 2, :], bank[0][:, 0:P], ACT.Copy).then_inc(s["ext"], 1)
                f(number[:, bass.ds(U * i + r, 1)], xt[:, r, D:D + 1], ACT.Copy).then_inc(s["numbered"], 1)

            def e_gelu(i, r):
                act.wait_ge(s["up1_ps"], U * i + r + 1)
                positive(act, s["prod_done"], U * i + r - 1)
                f(gel[:, r % 2, :], bank[3 + r % 2][:, :], ACT.Gelu).then_inc(s["gelu_done"], 1)

            def e_step(tile, before, behind):
                if behind is not None:
                    e_ext(*behind)
                e_gelu(*tile)

            e_ext(0, 0)
            e_step((0, 0), None, (0, 1))
            turns(act, e_step)

        @block.vector
        def _(dve):
            count = [0]

            def setup(ins):
                count[0] += 1
                ins.then_inc(s["dve_setup"], 1)
                dve.wait_ge(s["dve_setup"], count[0])

            def sign_and_floor(dst, src, t1, t2):
                setup(dve.tensor_scalar(t1, src, 0.0, 2.0, ALU.is_ge, ALU.mult))
                setup(dve.tensor_scalar(t1, t1, -1.0, None, ALU.add))
                setup(dve.tensor_tensor(t2, src, t1, ALU.mult))
                setup(dve.tensor_scalar(t2, t2, 0.25, None, ALU.max))
                setup(dve.tensor_tensor(dst, t1, t2, ALU.mult))

            setup(dve.memset(da[:, :, :, :, :], 0.0))
            setup(dve.memset(xpad[:, :, :, 0:K - 1], 0.0))
            dve.wait_ge(s["mod_ps"], 1)
            setup(dve.tensor_copy(mods[:, :, :], Y[0][:, 0:6 * B].rearrange("p (m b) -> p m b", m=6)))
            setup(dve.tensor_copy(gate_t1[:, :], Y[0][0:B, P:P + D]))
            sign_and_floor(gate16[:, :], gate_t1[:, :], gate_t3[:, :], gate_t2[:, :])
            for m in (1, 4):
                setup(dve.tensor_scalar(mods[:, m, :], mods[:, m, :], 1.0, None, ALU.add))
            sign_and_floor(mods[:, 2, :], mods[:, 2, :], mod_t1[:, :], mod_t2[:, :])
            dve.wait_ge(s["weights_in"], WEIGHTS)
            setup(dve.tensor_scalar(w_dt[:, :], w_dt[:, :], ln_dt[:, :], None, ALU.mult))
            dve.wait_ge(s["pool_setup"], POOL_SETUP)
            for h in range(H):
                setup(dve.tensor_scalar(d_diag[:, h, :], ident[:, :], d_skip[:, h:h + 1], None, ALU.mult))
            dve.wait_ge(s["exp_a"], 1)
            setup(dve.tensor_scalar(neg_a[:, :, :], neg_a[:, :, :], -1.0, None, ALU.mult))
            assert count[0] == DVE_SETUP
            for r in range(B // 4):
                dve.wait_ge(s["gate_ps"], r + 1)
                dve.tensor_copy(gate_b[:, 4 * r:4 * r + 4, :].rearrange("p b d -> p (b d)"), Y[(r + 1) % 2][:, :])\
                    .then_inc(s["gate_read"], 1)

            link_a = chained(dve, "a_dve", A_LINKS)
            link_c = chained(dve, "c_dve", C_LINKS)

            def aggregate(j, stats, mv, link, done):
                even, odd = (stats[:, :, k:k + 3].rearrange("p t k -> p k t") for k in (0, 3))
                dve.tensor_tensor(mv[:, 0, :], even[:, 1], odd[:, 1], ALU.add)
                dve.tensor_tensor(mv[:, 1, :], even[:, 2], odd[:, 2], ALU.add)
                link(j, dve.tensor_tensor(mv[:, 2, :], even[:, 1], odd[:, 1], ALU.subtract))
                dve.tensor_scalar(mv[:, 0, :], mv[:, 0, :], -0.5, None, ALU.mult)
                link(j, dve.tensor_tensor(mv[:, 2, :], mv[:, 2, :], mv[:, 2, :], ALU.mult))
                dve.scalar_tensor_tensor(mv[:, 1, :], mv[:, 2, :], D / 4.0, mv[:, 1, :], ALU.mult, ALU.add).then_inc(s[done], 1)

            def a_stats(j):
                if isinstance(j, int) and j == 0:
                    dve.wait_ge(s["x_first_in"], 16)
                else:
                    dve.wait_ge(s["x_rest_in"], 16 * (G - 1))
                    dve.wait_ge(s["a_h"], j)
                dve.tensor_copy(a_mod[:, :, :], mods[:, 0:2, bass.ds(GB * j, GB)])
                for t in range(TG):
                    last = dve.bn_stats(stats_a[:, t, :], x_all[:, bass.ds(j * TG + t, 1), :].rearrange("p o d -> p (o d)"))
                link_a(j, last)
                aggregate(j, stats_a, mv_a, link_a, "a_mv")

            def shift(j, mv, rstd, chain):
                dve.wait_ge(s[chain + "_rstd"], j + 1)
                dve.tensor_tensor(mv[:, 2, :], mv[:, 0, :], rstd[:, :], ALU.mult).then_inc(s[chain + "_shift"], 1)

            def a_hn(j, q):
                dve.wait_ge(s["a_rms"], j + 1)
                dve.scalar_tensor_tensor(hn, h_t[:, q, :], ln_in[:, :], rms_a, ALU.mult, ALU.mult).then_inc(s["a_hn"], 1)

            def a_conv(j, taps):
                for k in taps:
                    for h in range(H):
                        if k == 0:
                            dve.wait_ge(s["a_xpad"], H * j + h + 1)
                        last = dve.scalar_tensor_tensor(conv[:, h], xpad[:, h, :, k:k + S], conv_w[:, h, k:k + 1], conv[:, h],
                                                        ALU.mult, ALU.add)
                    if k < K - 2:
                        link_a(j, last)
                    else:
                        last.then_inc(s["a_conv"], 1)

            def a_ms(j):
                dve.wait_ge(s["a_proj_copy"], j + 1)
                dve.tensor_reduce(proj_ms[:, 0, :], proj_sq[:, :, 0:R], AX, ALU.add)
                dve.tensor_reduce(proj_ms[:, 1:3, :].rearrange("p s t -> p t s"),
                                  proj_sq[:, :, R:XP].rearrange("p t (s n) -> p t s n", s=2), AX, ALU.add)\
                    .then_inc(s["a_proj_ms"], 1)

            def a_parts(j):
                dve.wait_ge(s["a_proj_rs"], j + 1)
                link_a(j, dve.tensor_tensor(bcn.rearrange("p t (s n) -> p t s n", s=2),
                                            proj[:, :, R:XP].rearrange("p t (s n) -> p t s n", s=2),
                                            proj_rs[:, 1:3, :].rearrange("p s t -> p t s").unsqueeze(3)
                                            .broadcast_to([P, TG, 2, NS]), ALU.mult))
                ln = ln_bc[:, :].unsqueeze(1).broadcast_to([P, TG, BC])
                dve.tensor_tensor(dtc[:, :, R:R + NS], bcn[:, :, NS:BC], ln[:, :, NS:BC], ALU.mult)
                dve.tensor_tensor(dtc[:, :, 0:R], proj[:, :, 0:R], proj_rs[:, 0, :].unsqueeze(2).broadcast_to([P, TG, R]),
                                  ALU.mult).then_inc(s["a_dtn"], 1)
                rest = bcn[:, :, 0:NS]
                link_a(j, dve.tensor_tensor(rest, rest, ln[:, :, 0:NS], ALU.mult))
                for k in range(2):
                    piece = parts_tok[:, :, k * NS:(k + 1) * NS]
                    link_a(j, dve.tensor_copy(piece, rest))
                    link_a(j, dve.tensor_tensor(rest, rest, piece, ALU.subtract))
                dve.tensor_copy(parts_tok[:, :, 2 * NS:3 * NS], rest).then_inc(s["a_parts"], 1)

            def a_u(j, q):
                dve.wait_ge(s["a_soft"], j + 1)
                dve.tensor_tensor(dt[:, q], soft, relu, ALU.add).then_inc(s["dt_ready"], 1)
                dve.wait_ge(s["dt_ready"], j + 1)
                dve.tensor_tensor(u[:, q], dt[:, q], xs_[:, q], ALU.mult).then_inc(s["u_ready"], 1)

            def c_y(j, q):
                dve.wait_ge(s["nsum_done"], (j + 1) * NS)
                dve.tensor_copy(c_mod[:, :, :], mods[:, :, bass.ds(GB * j, GB)])
                for h in range(H):
                    last = dve.tensor_tensor(yt[:, h, :], Y[h][:, :], zs[:, q, h, :], ALU.mult)
                last.then_inc(s["yg_ready"], 1)

            def c_hn(j):
                dve.wait_ge(s["c_rms"], j + 1)
                dve.scalar_tensor_tensor(tmp_c[:, :], hid[:, :], ln_moe[:, :], rms_c[:, :], ALU.mult, ALU.mult)\
                    .then_inc(s["c_hn"], 1)

            def c_product(j, first, k, acted, done):
                dve.wait_ge(s[acted], j * FC + k + 1)
                filled(dve, "c", C_FREED, first + 2 * k + 1, j)
                dve.tensor_tensor(prod_c[:, k, :], act_c[:, k % 2, :], CW[1][:, :], ALU.mult).then_inc(s[done], 1)

            def c_dense_product(j, k):
                c_product(j, C_FFN, k, "c_silu", "c_prod")

            def c_expert_product(j, k):
                c_product(j, C_SHARED_FFN, k, "c_gelu", "c_sprod")

            def group_of(j):
                return x_all[:, bass.ds(j * TG, TG), :]

            def c_x2(j):
                filled(dve, "c", C_FREED, C_OGT, j)
                dve.tensor_tensor(group_of(j), CW[1][:, :].rearrange("p (t d) -> p t d", t=TG), group_of(j), ALU.add)\
                    .then_inc(s["x2_ready"], 1)
                apart(dve)
                dve.wait_ge(s["x2_ready"], j + 1)
                for t in range(TG):
                    last = dve.bn_stats(stats_c[:, t, :], x_all[:, bass.ds(j * TG + t, 1), :].rearrange("p o d -> p (o d)"))
                link_c(j, last)
                aggregate(j, stats_c, mv_c, link_c, "c_mv")

            def over_e(a):
                return a.unsqueeze(2).broadcast_to([P, TG, NE])

            def c_onehot(j):
                filled(dve, "c", C_FREED, C_LOGIT, j)
                lg = CW[0][:, 0:TG * NE].rearrange("p (t e) -> p t e", t=TG)
                link_c(j, dve.tensor_reduce(lmax[:, :], lg, AX, ALU.max))
                dve.tensor_tensor(eq[:, :, :], lg, over_e(lmax[:, :]), ALU.is_equal).then_inc(s["c_eq"], 1)
                dve.wait_ge(s["c_eq"], j + 1)
                link_c(j, dve.tensor_tensor(eq[:, :, :], eq[:, :, :], rev[:, :].unsqueeze(1).broadcast_to([P, TG, NE]), ALU.mult))
                link_c(j, dve.tensor_reduce(emax[:, :], eq[:, :, :], AX, ALU.max))
                dve.tensor_tensor(onehot[:, :, :], eq[:, :, :], over_e(emax[:, :]), ALU.is_equal).then_inc(s["c_onehot"], 1)

            def c_slots(j):
                filled(dve, "c", C_FREED, C_RANK, j)
                dve.tensor_copy(counted[:, :, :, :].rearrange("p k t e -> p (k t e)"), CW[1][:, 0:2 * TG * NE])\
                    .then_inc(s["c_counts"], 1)
                dve.wait_ge(s["c_counts"], j + 1)
                w = counted
                link_c(j, dve.tensor_copy(base5[:, 0, :], base5[:, TG, :]))
                for t in range(TG):
                    link_c(j, dve.tensor_tensor(base5[:, t + 1, :], base5[:, t, :], w[:, 1, t, :], ALU.add))
                dve.tensor_tensor(rk[:, :, :], w[:, 0], base5[:, 0:TG, :], ALU.add).then_inc(s["c_ranked"], 1)
                dve.wait_ge(s["c_ranked"], j + 1)
                link_c(j, dve.tensor_tensor(rk[:, :, :], rk[:, :, :], onehot[:, :, :], ALU.mult))
                link_c(j, dve.tensor_reduce(rank[:, :], rk[:, :, :], AX, ALU.add))
                link_c(j, dve.tensor_scalar(slot_f[:, :], emax[:, :], -float(REG), float(NE * REG), ALU.mult, ALU.add))
                link_c(j, dve.tensor_tensor(slot_f[:, :], slot_f[:, :], rank[:, :], ALU.add))
                positive(dve, s["scattered"], 16 * TG * j)
                dve.tensor_copy(h2_tok[:, :, D:D + 1].rearrange("p t o -> p (t o)"), token[:, bass.ds(j * TG, TG)])
                dve.tensor_copy(slot[:, :], slot_f[:, :]).then_inc(s["c_slot"], 1)

            def c_base(j):
                filled(dve, "c", C_FREED, C_SHARED, j)
                g4 = gate_b[:, bass.ds(GB * j, GB), :].unsqueeze(2).broadcast_to([P, GB, TG // GB, D])
                dve.tensor_tensor(rms_c[:, :].rearrange("p (b t d) -> p b t d", b=GB, d=D),
                                  CW[0][:, :].rearrange("p (b t d) -> p b t d", b=GB, d=D), g4, ALU.mult).then_inc(s["c_gated"], 1)
                dve.wait_ge(s["c_gated"], j + 1)
                dve.tensor_tensor(group_of(j), rms_c[:, :].rearrange("p (t d) -> p t d", t=TG), group_of(j), ALU.add)\
                    .then_inc(s["base_ready"], 1)

            def scan_input(g, q, n):
                if n == 0:
                    dve.wait_ge(s["u_ready"], g + 1)
                dve.wait_ge(s["b_full"], g * NS + n + 1)
                positive(dve, s["h_done"], g * NS + n - RING_X + 1)
                dve.tensor_tensor(bx[:, n % RING_X], u[:, q], BB[n % 2][:, :].unsqueeze(1).broadcast_to([P, H, GT]), ALU.mult)\
                    .then_inc(s["bx_done"], 1)

            def product(g, n):
                if n in POOL_N:
                    return
                wait_c(dve, g, n)
                dve.wait_ge(s["h_done"], g * NS + n + 1)
                positive(dve, s["nsum_done"], g * NS + n - RING_P + 1)
                dve.tensor_tensor(hc[:, n % RING_P], hs[:, n % RING_H],
                                  cs[:, n % RING_C].unsqueeze(1).broadcast_to([P, H, GT]), ALU.mult)\
                    .then_inc(s["hc_dve"], 1)

            def scan(g, n):
                dve.wait_ge(s["bx_done"], g * NS + n + 1)
                dve.wait_ge(s["da_ready"], g * NS + n + 1)
                wait_hc(dve, back(g, n, RING_H))
                dve.tensor_tensor_scan(hs[:, n % RING_H].rearrange("p h t -> p (h t)"),
                                       da[:, n % RING_A].rearrange("p h b t -> p (h b t)"),
                                       bx[:, n % RING_X].rearrange("p h t -> p (h t)"), 0.0, ALU.mult, ALU.add)\
                    .then_inc(s["h_done"], 1)

            def steps(n, g, q, has_scan, has_a, has_c):
                ja, qa, jc = g + 1, 1 - q, g - 1

                def a(part, *args):
                    if has_a:
                        part(ja, *args)

                def c(part, *args):
                    if has_c:
                        part(jc, *args)

                if has_scan:
                    if n + 1 < NS:
                        scan_input(g, q, n + 1)
                    elif has_a:
                        scan_input(ja, qa, 0)
                    scan(g, n)
                if n in (6, 7):
                    c(c_dense_product, 2 * (n - 6))
                elif n == 12:
                    c(c_onehot)
                elif n in (13, 14):
                    c(c_expert_product, 2 * (n - 13))
                if has_scan and back(g, n, 1) is not None:
                    product(*back(g, n, 1))
                if n == 0:
                    a(a_stats)
                elif n == 1:
                    c(c_y, qa), a(shift, mv_a, rstd_a, "a")
                elif n == 4:
                    a(a_hn, qa), c(c_hn)
                elif n == 5:
                    a(a_conv, (0,))
                elif n == 6:
                    c(c_dense_product, 1), a(a_conv, (1, 2))
                elif n == 7:
                    c(c_dense_product, 3)
                elif n == 8:
                    a(a_ms)
                elif n == 9:
                    a(a_parts), c(c_x2)
                elif n == 10:
                    c(shift, mv_c, rstd_c, "c")
                elif n == 12:
                    c(c_slots)
                elif n == 13:
                    c(c_expert_product, 1), a(a_u, qa)
                elif n == 14:
                    c(c_expert_product, 3)
                elif n == 15:
                    c(c_base)

            def body(g, q, has_a, has_c):
                for n in range(NS):
                    steps(n, g, q, True, has_a, has_c)

            for n in range(NS):
                steps(n, -1, 1, False, True, False)
            scan_input(0, 0, 0)
            dve.wait_ge(s["zeros_out"], 16)
            groups(dve, body)
            product(G - 1, NS - 1)
            for n in range(NS):
                steps(n, G, 0, False, False, True)

            link_e = chained(dve, "e_dve", 10 ** 6)
            link = lambda ins: link_e(0, ins)
            tt = dve.tensor_tensor
            counts = base5[:, TG, :]
            link(tt(tail_f[:, :], counts, region[:, :], ALU.add))
            link(dve.tensor_scalar(tail_f[:, :], tail_f[:, :], pid[:, :], None, ALU.add))
            dve.tensor_copy(tail[:, :], tail_f[:, :]).then_inc(s["tail_idx"], 1)
            k_big = big[:, 0:NT, :]
            link(tt(k_big, counts.unsqueeze(1).broadcast_to([P, NT, NE]), iota_k[:, 0:NT].unsqueeze(2).broadcast_to([P, NT, NE]), ALU.is_gt))
            link(dve.tensor_reduce(n_tiles[:, :], k_big.rearrange("p k e -> p e k"), AX, ALU.add))
            link(dve.tensor_tensor_scan(last_tile[:, :], ones8[:, :], n_tiles[:, :], 0.0, ALU.mult, ALU.add))
            each = [P, TILES, NE]
            link(tt(big[:, :, :], iota_j[:, 0:TILES].unsqueeze(2).broadcast_to(each), last_tile[:, :].unsqueeze(1).broadcast_to(each), ALU.is_ge))
            link(dve.tensor_reduce(ej[:, :], big[:, :, :], AX, ALU.add))
            link(tt(big[:, :, :], big[:, :, :], n_tiles[:, :].unsqueeze(1).broadcast_to(each), ALU.mult))
            link(dve.tensor_reduce(kj[:, :], big[:, :, :], AX, ALU.add))
            link(tt(kj[:, :], iota_j[:, 0:TILES], kj[:, :], ALU.subtract))
            link(dve.tensor_scalar(kj[:, :], kj[:, :], float(P), None, ALU.mult))
            link(dve.scalar_tensor_tensor(rowf[:, :], ej[:, :], float(REG), kj[:, :], ALU.mult, ALU.add))
            link(dve.tensor_scalar(ej[:, :], ej[:, :], float(NE - 1), None, ALU.min))
            dve.tensor_copy(row_tab[:, :], rowf[:, :])
            dve.tensor_copy(exp_tab[:, :], ej[:, :]).then_inc(s["tables"], 1)

            def e_product(i, r):
                dve.wait_ge(s["gelu_done"], U * i + r + 1)
                dve.wait_ge(s["up2_ps"], U * i + r + 1)
                positive(dve, s["prodt_ps"], U * i + r - 1)
                tt(pe_[:, r % 2, :], gel[:, r % 2, :], bank[5 + r % 2][:, :], ALU.mult).then_inc(s["prod_done"], 1)

            def e_prod_t(i, r):
                dve.wait_ge(s["prodt_ps"], U * i + r + 1)
                dve.tensor_copy(pet[:, r % 2, :], bank[1][:, :]).then_inc(s["prodt"], 1)

            def e_out(i, r):
                dve.wait_ge(s["down_ps"], U * i + r + 1)
                positive(dve, s[f"ys_out{r % 2}"], 16 * (U // 2 * i + r // 2))
                dve.tensor_copy(yo[:, r % 2, :], bank[2][:, 0:D]).then_inc(s["yo"], 1)

            def e_step(tile, before, behind):
                e_prod_t(*before)
                e_product(*tile)
                e_out(*before)

            e_product(0, 0)
            turns(dve, e_step)
            e_prod_t(*LAST)
            e_out(*LAST)

            for j in range(G):
                rows = y_rows[:, j * TG:(j + 1) * TG, :]
                dve.wait_ge(s[f"gathered{j}"], 16)
                g4 = gate_b[:, GB * j:GB * (j + 1), :].unsqueeze(2).broadcast_to([P, GB, TG // GB, D])
                tt(rows.rearrange("p (b t) d -> p b t d", b=GB), rows.rearrange("p (b t) d -> p b t d", b=GB), g4, ALU.mult)\
                    .then_inc(s["weighted"], 1)
                dve.wait_ge(s["weighted"], j + 1)
                tt(x_all[:, j * TG:(j + 1) * TG, :], x_all[:, j * TG:(j + 1) * TG, :], rows, ALU.add).then_inc(s["final_sum"], 1)


_INS = ["L0_attn_hidden_states", "L0_attn_in_proj_w", "L0_attn_conv_w", "L0_attn_conv_b", "L0_attn_x_proj_w",
        "L0_attn_dt_proj_w", "L0_attn_dt_proj_b", "L0_attn_dt_ln_w", "L0_attn_b_ln_w", "L0_attn_c_ln_w", "L0_attn_A_log",
        "L0_attn_D_skip", "L0_attn_out_proj_w", "L0_attn_input_ln_w", "L0_attn_pre_moe_ln_w", "L0_attn_gate_w",
        "L0_attn_up_w", "L0_attn_down_w", "L0_ffn_w1s", "L0_ffn_w2s", "L0_ffn_w3s", "L0_ffn_W1", "L0_ffn_W2", "L0_ffn_W3",
        "L0_ffn_Wg", "L0_c", "L0_wmod"]

_BY_HALF = ("L0_attn_conv_b", "L0_attn_dt_proj_b", "L0_attn_D_skip")


def kernel(**inputs):
    import numpy as _np
    import concourse.bacc as _bacc
    from concourse import mybir as _mybir
    from concourse.bass_utils import run_bass_kernel_spmd as _run

    nc = _bacc.Bacc("TRN2", target_bir_lowering=False, num_devices=1)
    arrays, io = {}, {}
    for name in _INS:
        a = _np.asarray(inputs[name])
        if name in _BY_HALF:
            a = a.reshape(H, P).T
        a = _np.ascontiguousarray(a)
        arrays[f"in_{name}"] = a
        io[name] = nc.dram_tensor(f"in_{name}", a.shape, _mybir.dt.from_np(a.dtype), kind="ExternalInput").ap()
    out = nc.dram_tensor("out_0", (B, S, D), _mybir.dt.float32, kind="ExternalOutput").ap()
    build(nc, io, out)
    r = _run(nc, [arrays], core_ids=[0])
    return r.results[0]["out_0"]
```
